# Optimizing a Trainium2 kernel written in Bass

```python
import numpy as np
import jax
import jax.numpy as jnp

def _softmax(x, axis=-1):
    return jax.nn.softmax(x, axis=axis)

def _gelu(x):
    return jax.nn.gelu(x, approximate=True)

def _silu(x):
    return jax.nn.silu(x)

def _sigmoid(x):
    return jax.nn.sigmoid(x)

def _layernorm(x, axis=-1, eps=1e-05):
    m = jnp.mean(x, axis=axis, keepdims=True)
    v = jnp.var(x, axis=axis, keepdims=True)
    return (x - m) / jnp.sqrt(v + eps)

def _scatter_add(tgt, idx, src, axis=0):
    return tgt.at[idx].add(src)

def _segment_sum(src, seg, n):
    return jax.ops.segment_sum(src, seg, n)
kernel_name = 'mk_seq_preln_d1_jaxref_r4_ae2892'

def setup_inputs(seed: int=0):
    np.random.seed(seed)
    _w = jnp.asarray

    def _L0_attn_setup():
        import jax, jax.numpy as jnp
        import numpy as np
        import math
        LN_EPS = 1e-05

        def _layernorm(h, gamma, beta):
            mu = jnp.mean(h, axis=-1, keepdims=True)
            var = jnp.var(h, axis=-1, keepdims=True)
            return (h - mu) * jax.lax.rsqrt(var + LN_EPS) * gamma + beta
        key = jax.random.key(seed)
        ks = jax.random.split(key, 6)
        B, S, D = (4, 1024, 256)
        x = jax.random.normal(ks[0], (B, S, D), dtype=jnp.float32)
        W_omega = jax.random.normal(ks[1], (D, D), dtype=jnp.float32) / math.sqrt(D)
        b_omega = jnp.zeros((D,), dtype=jnp.float32)
        log_scale = jnp.full((D,), math.log(0.1), dtype=jnp.float32)
        ln_gamma = jnp.ones((4 * D,), dtype=jnp.float32)
        ln_beta = jnp.zeros((4 * D,), dtype=jnp.float32)
        W1 = jax.random.normal(ks[2], (2 * D, 4 * D), dtype=jnp.float32) / math.sqrt(4 * D)
        b1 = jnp.zeros((2 * D,), dtype=jnp.float32)
        W2 = jax.random.normal(ks[3], (D, 2 * D), dtype=jnp.float32) / math.sqrt(2 * D)
        b2 = jnp.zeros((D,), dtype=jnp.float32)
        return {'x': x, 'W_omega': W_omega, 'b_omega': b_omega, 'log_scale': log_scale, 'ln_gamma': ln_gamma, 'ln_beta': ln_beta, 'W1': W1, 'b1': b1, 'W2': W2, 'b2': b2}
    _L0_attn_in = _L0_attn_setup()

    def _L0_ffn_setup():
        import jax, jax.numpy as jnp
        import numpy as np
        EPS = 1e-05

        def _quantize(W):
            gamma = jnp.mean(jnp.abs(W))
            return jnp.clip(jnp.round(W / (gamma + EPS)), -1.0, 1.0)
        key = jax.random.key(seed)
        k_x, k_w1, k_b1, k_w2, k_b2 = jax.random.split(key, 5)
        n_embd = 256
        d_ff = 4 * n_embd
        B, S = (4, 1024)
        bound1 = 1.0 / np.sqrt(n_embd)
        bound2 = 1.0 / np.sqrt(d_ff)
        x = jax.random.normal(k_x, (B, S, n_embd), dtype=jnp.float32)
        W1 = jax.random.uniform(k_w1, (d_ff, n_embd), jnp.float32, -bound1, bound1)
        b1 = jax.random.uniform(k_b1, (d_ff,), jnp.float32, -bound1, bound1)
        W2 = jax.random.uniform(k_w2, (n_embd, d_ff), jnp.float32, -bound2, bound2)
        b2 = jax.random.uniform(k_b2, (n_embd,), jnp.float32, -bound2, bound2)
        return {'x': x, 'W1': W1, 'b1': b1, 'W2': W2, 'b2': b2}
    _L0_ffn_in = _L0_ffn_setup()
    _d = {'L0_attn_x': _L0_attn_in['x'], 'L0_attn_W_omega': _L0_attn_in['W_omega'], 'L0_attn_b_omega': _L0_attn_in['b_omega'], 'L0_attn_log_scale': _L0_attn_in['log_scale'], 'L0_attn_ln_gamma': _L0_attn_in['ln_gamma'], 'L0_attn_ln_beta': _L0_attn_in['ln_beta'], 'L0_attn_W1': _L0_attn_in['W1'], 'L0_attn_b1': _L0_attn_in['b1'], 'L0_attn_W2': _L0_attn_in['W2'], 'L0_attn_b2': _L0_attn_in['b2'], 'L0_ffn_W1': _L0_ffn_in['W1'], 'L0_ffn_b1': _L0_ffn_in['b1'], 'L0_ffn_W2': _L0_ffn_in['W2'], 'L0_ffn_b2': _L0_ffn_in['b2']}
    _x0 = _d['L0_attn_x']
    _d['L0_attn_x'] = jax.random.normal(jax.random.fold_in(jax.random.key(seed), 1), (16, 1024, 256), dtype=_x0.dtype)
    del _x0
    return _d

def reference(L0_attn_x, L0_attn_W_omega, L0_attn_b_omega, L0_attn_log_scale, L0_attn_ln_gamma, L0_attn_ln_beta, L0_attn_W1, L0_attn_b1, L0_attn_W2, L0_attn_b2, L0_ffn_W1, L0_ffn_b1, L0_ffn_W2, L0_ffn_b2):

    def _L0_attn_ref(x, W_omega, b_omega, log_scale, ln_gamma, ln_beta, W1, b1, W2, b2):
        import jax, jax.numpy as jnp
        import numpy as np
        import math
        LN_EPS = 1e-05

        def _layernorm(h, gamma, beta):
            mu = jnp.mean(h, axis=-1, keepdims=True)
            var = jnp.var(h, axis=-1, keepdims=True)
            return (h - mu) * jax.lax.rsqrt(var + LN_EPS) * gamma + beta
        B, S, D = x.shape
        omega = jnp.einsum('bsd,ed->bse', x, W_omega) + b_omega
        position = jnp.arange(1, S + 1, dtype=x.dtype).reshape(1, S, 1)
        pos_scale = 1.0 / jnp.sqrt(position)
        omega_scaled = omega * jnp.exp(log_scale) * pos_scale
        phi = jnp.cumsum(omega_scaled, axis=1)
        cos_phi = jnp.cos(phi)
        sin_phi = jnp.sin(phi)
        cm_real = x * cos_phi
        cm_imag = x * sin_phi
        mem_real = jnp.cumsum(cm_real, axis=1) / position
        mem_imag = jnp.cumsum(cm_imag, axis=1) / position
        ret_real = mem_real * cos_phi + mem_imag * sin_phi
        ret_imag = mem_imag * cos_phi - mem_real * sin_phi
        context = jnp.concatenate([cm_real, cm_imag, ret_real, ret_imag], axis=-1)
        h = _layernorm(context, ln_gamma, ln_beta)
        h = jnp.einsum('bsd,ed->bse', h, W1) + b1
        h = jax.nn.gelu(h, approximate=False)
        h = jnp.einsum('bsd,ed->bse', h, W2) + b2
        return x + h

    def _L0_ffn_ref(x, W1, b1, W2, b2):
        import jax, jax.numpy as jnp
        import numpy as np
        EPS = 1e-05

        def _quantize(W):
            gamma = jnp.mean(jnp.abs(W))
            return jnp.clip(jnp.round(W / (gamma + EPS)), -1.0, 1.0)
        Wq1 = _quantize(W1)
        Wq2 = _quantize(W2)
        h = jax.nn.relu(jnp.einsum('bsd,fd->bsf', x, Wq1) + b1)
        out = jnp.einsum('bsf,df->bsd', h, Wq2) + b2
        return out
    x = L0_attn_x
    x = x + _L0_attn_ref(_layernorm(x, axis=-1), L0_attn_W_omega, L0_attn_b_omega, L0_attn_log_scale, L0_attn_ln_gamma, L0_attn_ln_beta, L0_attn_W1, L0_attn_b1, L0_attn_W2, L0_attn_b2)
    x = x + _L0_ffn_ref(_layernorm(x, axis=-1), L0_ffn_W1, L0_ffn_b1, L0_ffn_W2, L0_ffn_b2)
    return x

_drawn_inputs = setup_inputs


def setup_inputs(seed=0):
    import zlib

    import numpy as np

    out = dict(_drawn_inputs(seed))
    spreads = {'L0_attn_b_omega': (0.0, 0.1),
     'L0_attn_log_scale': (-2.3025851249694824, 0.2),
     'L0_attn_ln_gamma': (1.0, 0.2),
     'L0_attn_ln_beta': (0.0, 0.1),
     'L0_attn_b1': (0.0, 0.1),
     'L0_attn_b2': (0.0, 0.1)}
    factors = {'L0_ffn_b1': 21.72, 'L0_ffn_b2': 64.0}
    for name, (base, spread) in spreads.items():
        noise = np.random.default_rng([zlib.crc32(name.encode()), seed]).standard_normal(out[name].shape)
        drawn = base * np.exp(spread * noise) if base else spread * noise
        out[name] = jnp.asarray(drawn.astype(out[name].dtype))
    for name, factor in factors.items():
        out[name] = (out[name] * factor).astype(out[name].dtype)
    return out
```

```python
from contextlib import ExitStack

import concourse.bass as bass
from concourse import mybir

ALU = mybir.AluOpType
ACT = mybir.ActivationFunctionType
AX = mybir.AxisListType
F32 = mybir.dt.float32
F16 = mybir.dt.float16
U32 = mybir.dt.uint32
ABSMAX = bass.bass_isa.ReduceOp.absmax

P = 128
EPS = 1e-5
PI = 3.141592653589793
LN_SCALE = 1024.0
ROUND = 12582912.0
TWO_PI = 6.283185
EXPONENT_BITS = 0x7F800000


def phase_mixer_layer(nc, x, w_omega, b_omega, log_scale, ln_gamma, ln_beta, w1, b1, w2, b2,
                      f_w1, f_b1, f_w2, f_b2, pos_table, out):
    BATCH, SEQ, D = x.shape
    E1, C = w1.shape
    F = f_w1.shape[0]
    CH = 512
    NT = CH // P
    CHUNKS = BATCH * SEQ // CH
    KD, KC, KE, KF = D // P, C // P, E1 // P, F // P
    PER_SEQ = SEQ // CH
    assert PER_SEQ == 2 and KD == 2 and C == 4 * D and KE == 4 and KF == 8
    SLOTS = 4
    LAG = 3
    LOOP_FROM, LOOP_TO = 2, CHUNKS - 4

    x_v = x.rearrange("b (c t p) d -> (b c) p t d", t=NT, p=P)
    out_v = out.rearrange("b (c t p) d -> (b c) p t d", t=NT, p=P)

    ctx = ExitStack()
    with ctx:
        def sb(name, shape, dt=F32):
            return ctx.enter_context(nc.sbuf_tensor(name, shape, dt))

        def sem(name):
            return ctx.enter_context(nc.semaphore(name))

        ident = sb("ident", [P, P])
        ones = sb("ones", [P, P])
        pos_rsqrt = sb("pos_rsqrt", [P, SEQ])
        pos_inv = sb("pos_inv", [P, SEQ])
        b2_rows = sb("b2_rows", [P, D])
        fb2_rows = sb("fb2_rows", [P, D])
        wo_hi = sb("wo_hi", [P, KD, D], F16)
        wo_lo = sb("wo_lo", [P, KD, D], F16)
        w1_hi = sb("w1_hi", [P, KC, E1], F16)
        w1_lo = sb("w1_lo", [P, KC, E1], F16)
        w2_hi = sb("w2_hi", [P, KE, D], F16)
        w2_lo = sb("w2_lo", [P, KE, D], F16)
        fw1_t = sb("fw1_t", [P, KD, F], F16)
        fw2_t = sb("fw2_t", [P, KF, D], F16)
        b_om = sb("b_om", [P, KD])
        lscale = sb("lscale", [P, KD])
        e_base = sb("e_base", [P, KD])
        exp_ls = sb("exp_ls", [P, KD])
        om_scale = sb("om_scale", [P, KD])
        om_bias = sb("om_bias", [P, KD])
        b1_raw = sb("b1_raw", [P, KE])
        b1_dot = sb("b1_dot", [P, KE])
        b1_full = sb("b1_full", [P, KE])
        row_mean = sb("row_mean", [P, KE])
        fb1 = sb("fb1", [P, KF])
        relu_bias = sb("relu_bias", [P, KF])
        half_pi = sb("half_pi", [P, 1])
        minus_half = sb("minus_half", [P, NT])
        mags = sb("mags", [P, 5])
        mags_all = sb("mags_all", [P, 5])
        pw = sb("pw", [P, 5])
        up = sb("up", [P, 5])
        down = sb("down", [P, 5])
        h_down = sb("h_down", [P, 1])
        relu_scale = sb("relu_scale", [P, 1])
        abs_sums = sb("abs_sums", [P, 2])
        thr = sb("thr", [P, 2])
        neg_thr = sb("neg_thr", [P, 2])

        x_rows = sb("x_rows", [P, 2, NT, D])
        base = sb("base", [P, 2, NT, D])
        x1 = sb("x1", [P, 2, NT, D])
        xs = sb("xs", [P, NT, D])
        xs2 = sb("xs2", [P, NT, D])
        bn1 = sb("bn1", [P, NT, 6])
        mv1 = sb("mv1", [P, 2, NT, 2])
        ve1 = sb("ve1", [P, NT])
        rs1 = sb("rs1", [P, 2, NT])
        gain1 = sb("gain1", [P, 2, NT])
        shift1 = sb("shift1", [P, 2, NT])
        sq1 = sb("sq1", [P, 2, NT])
        bn2 = sb("bn2", [P, NT, 6])
        mv2 = sb("mv2", [P, NT, 2])
        ve2 = sb("ve2", [P, NT])
        rs2 = sb("rs2", [P, NT])
        cmu = sb("cmu", [P, NT])
        cmu2 = sb("cmu2", [P, NT])
        csq = sb("csq", [P, NT])
        cvar = sb("cvar", [P, NT])
        cve = sb("cve", [P, NT])
        crs = sb("crs", [P, NT])
        diag = sb("diag", [P, NT, P])

        xf = sb("xf", [P, KD, CH])
        xh = sb("xh", [P, KD, CH], F16)
        xl = sb("xl", [P, KD, CH], F16)
        ph = sb("ph", [P, KD, CH])
        ph_carry = sb("ph_carry", [P, KD, 1])
        turn = sb("turn", [P, KD, CH])
        sn = sb("sn", [P, KD, CH])
        cs = sb("cs", [P, KD, CH])
        cmr = sb("cmr", [P, KD, CH])
        cmi = sb("cmi", [P, KD, CH])
        mr = sb("mr", [P, KD, CH])
        mi = sb("mi", [P, KD, CH])
        mr_carry = sb("mr_carry", [P, KD, 1])
        mi_carry = sb("mi_carry", [P, KD, 1])
        rr = sb("rr", [P, KD, CH])
        ri = sb("ri", [P, KD, CH])
        qa = sb("qa", [P, KD, CH])
        qb = sb("qb", [P, KD, CH])
        sqr = sb("sqr", [P, KD, CH])
        rb = sb("rb", [P, CH])
        h2 = sb("h2", [P, KD, CH], F16)
        l2 = sb("l2", [P, KD, CH], F16)
        rh = sb("rh", [P, SLOTS, CH], F16)
        rl = sb("rl", [P, SLOTS, CH], F16)
        KB = 256
        arena = sb("arena", [P, 56 * KB])
        ch = arena[:, 0:16 * KB].bitcast(F16).rearrange("p (b k n) -> p b k n", b=2, k=KC)
        cl = arena[:, 16 * KB:32 * KB].bitcast(F16).rearrange("p (b k n) -> p b k n", b=2, k=KC)
        z = arena[:, 32 * KB:40 * KB].rearrange("p (k n) -> p k n", k=KE)
        gh = arena[:, 40 * KB:44 * KB].bitcast(F16).rearrange("p (k n) -> p k n", k=KE)
        gl = arena[:, 44 * KB:48 * KB].bitcast(F16).rearrange("p (k n) -> p k n", k=KE)
        rf = arena[:, 48 * KB:56 * KB].rearrange("p (k n) -> p k n", k=SLOTS)
        w1_in = arena[:, 0:16 * KB].rearrange("p (m c) -> p m c", m=KE)
        gamma_rows = arena[:, 16 * KB:20 * KB]
        beta_rows = arena[:, 20 * KB:24 * KB]
        w_tmp = arena[:, 24 * KB:32 * KB]
        fw1_in = arena[:, 32 * KB:40 * KB].rearrange("p (m d) -> p m d", m=KF)
        fw2_in = arena[:, 40 * KB:48 * KB].rearrange("p (m f) -> p m f", m=KD)
        w2_in = arena[:, 48 * KB:52 * KB].rearrange("p (m f) -> p m f", m=KD)
        wo_in = arena[:, 52 * KB:54 * KB].rearrange("p (m d) -> p m d", m=KD)

        ps = ctx.enter_context(nc.psum_tensor("ps", [P, 8, CH], F32))
        ps_rows_a = ps[:, 0:2, :].rearrange("p b (t d) -> p (b t) d", d=D)
        ps_rows_b = ps[:, 4:6, :].rearrange("p b (t d) -> p (b t) d", d=D)

        p_vec = sem("p_vec")
        p_tab = sem("p_tab")
        p_wo = sem("p_wo")
        p_w1 = sem("p_w1")
        p_w2 = sem("p_w2")
        p_fw1 = sem("p_fw1")
        p_fw2 = sem("p_fw2")
        p_zero = sem("p_zero")
        p_ident = sem("p_ident")
        p_const = sem("p_const")
        p_ones = sem("p_ones")
        p_exp = sem("p_exp")
        p_abs = sem("p_abs")
        p_mean = sem("p_mean")
        p_dve = sem("p_dve")
        p_fold = sem("p_fold")
        p_mags = sem("p_mags")
        p_max = sem("p_max")
        p_scales = sem("p_scales")
        p_tern = sem("p_tern")
        p_turned = sem("p_turned")
        p_hi = sem("p_hi")
        p_lo = sem("p_lo")
        p_plain = sem("p_plain")

        x_loaded = [sem(f"x_loaded{i}") for i in range(2)]
        stored = [sem(f"stored{i}") for i in range(2)]
        bn1_done, mv1_done, ve1_done = sem("bn1_done"), sem("mv1_done"), sem("ve1_done")
        rs1_done, xs_done, gain_done = sem("rs1_done"), sem("xs_done"), sem("gain_done")
        sq1a_done, sq1_done = sem("sq1a_done"), sem("sq1_done")
        scaled_done, base_done = sem("scaled_done"), sem("base_done")
        t1_done, xf_done, xh_done, xl_done = sem("t1_done"), sem("xf_done"), sem("xh_done"), sem("xl_done")
        omega_done, w_done, u_done, y_done = sem("omega_done"), sem("w_done"), sem("u_done"), sem("y_done")
        ycarry_done, turn_done, frac_done = sem("ycarry_done"), sem("turn_done"), sem("frac_done")
        abs_done, sin_done, cos_done = sem("abs_done"), sem("sin_done"), sem("cos_done")
        cmr_done, cmi_done = sem("cmr_done"), sem("cmi_done")
        sumr_done, sumi_done = sem("sumr_done"), sem("sumi_done")
        rcarry_done, icarry_done = sem("rcarry_done"), sem("icarry_done")
        mr_done, mi_done = sem("mr_done"), sem("mi_done")
        qa_done, qb_done, ra_done, rb_done = sem("qa_done"), sem("qb_done"), sem("ra_done"), sem("rb_done")
        rr_done, ri_done = sem("rr_done"), sem("ri_done")
        ch_done = [sem(f"ch_done{i}") for i in range(4)]
        cl_done = [sem(f"cl_done{i}") for i in range(4)]
        sqr_done, sqi_done, q2_done, q_done = sem("sqr_done"), sem("sqi_done"), sem("q2_done"), sem("q_done")
        s2_done, s3_done, s4_done, s_done = sem("s2_done"), sem("s3_done"), sem("s4_done"), sem("s_done")
        stats_done, cmu_done, cmu2_done = sem("stats_done"), sem("cmu_done"), sem("cmu2_done")
        csq_done, cvar_done, cve_done, crs_done = sem("csq_done"), sem("cvar_done"), sem("cve_done"), sem("crs_done")
        diag_done, spread_done, rbs_done = sem("diag_done"), sem("spread_done"), sem("rbs_done")
        w1_done = [sem(f"w1_done{m}") for m in range(KE)]
        z_done = [sem(f"z_done{m}") for m in range(KE)]
        g_done = [sem(f"g_done{m}") for m in range(KE)]
        gh_done = [sem(f"gh_done{m}") for m in range(KE)]
        gl_done = [sem(f"gl_done{m}") for m in range(KE)]
        w2_done, x1_done = sem("w2_done"), sem("x1_done")
        bn2_done, mv2_done, ve2_done = sem("bn2_done"), sem("mv2_done"), sem("ve2_done")
        rs2_done, xs2_done, xb_done = sem("rs2_done"), sem("xs2_done"), sem("xb_done")
        t2_done, h2_done, l2_done = sem("t2_done"), sem("h2_done"), sem("l2_done")
        f1_done = [sem(f"f1_done{m}") for m in range(SLOTS)]
        relu_done = [sem(f"relu_done{m}") for m in range(SLOTS)]
        rh_done = [sem(f"rh_done{m}") for m in range(SLOTS)]
        rl_done = [sem(f"rl_done{m}") for m in range(SLOTS)]
        f2_done = [sem(f"f2_done{m}") for m in range(SLOTS)]
        out_done = sem("out_done")

        class Counts:
            def __init__(self, eng, even):
                self.eng, self.even, self.held = eng, even, {}
                if not isinstance(even, int):
                    for plus in range(-1, 7):
                        self.value(1, plus)

            def value(self, times, plus):
                if isinstance(self.even, int):
                    return times * self.even + plus
                if (times, plus) not in self.held:
                    self.held[times, plus] = self.eng.snap(self.eng.to_reg(self.even * times + plus))
                return self.held[times, plus]

        class Step:
            def __init__(self, counts, odd):
                self.counts, self.odd = counts, odd

            def chunk(self, ahead):
                c = Chunk(self.counts, self.odd + ahead)
                return c if c.exists() else None

        class Chunk:
            def __init__(self, counts, more):
                self.counts, self.more = counts, more
                self.index = counts.even + more
                self.b = more % 2

            def exists(self):
                return not isinstance(self.index, int) or 0 <= self.index < CHUNKS

        def wait(eng, s, value):
            if not isinstance(value, int) or value > 0:
                eng.wait_ge(s, value)

        def need(eng, s, c, back=0):
            wait(eng, s, c.counts.value(1, c.more + 1 - back))

        def need_dma(eng, pair, c, back=0):
            wait(eng, pair[c.b], c.counts.value(8, 8 * (c.more - c.b - back) + 16))

        def need_block(eng, sems, m, c, back=0):
            wait(eng, sems[m % SLOTS], c.counts.value(2, 2 * (c.more - back) + m // SLOTS + 1))

        def stand_alone(eng):
            eng.wait_ge(p_scales, 3)

        def run(eng, step, first):
            for s in range(first, LOOP_FROM):
                step(Step(Counts(eng, s - s % 2), s % 2))
            with eng.Fori(LOOP_FROM // 2, LOOP_TO // 2) as pair:
                counts = Counts(eng, pair * 2)
                step(Step(counts, 0))
                step(Step(counts, 1))
            for s in range(LOOP_TO, CHUNKS):
                step(Step(Counts(eng, s - s % 2), s % 2))

        groups = [([(wo_in, e, k) for k in range(KD) for e in range(KD)],
                   wo_hi[:, :, :].rearrange("p k e -> p (k e)"), wo_lo[:, :, :].rearrange("p k e -> p (k e)"), 0)]
        for k in range(0, KF, 2):
            groups.append(([(fw2_in, m, k + i) for i in range(2) for m in range(KD)],
                           fw2_t[:, k:k + 2, :].rearrange("p k e -> p (k e)"), None, None))
        for k in range(KD):
            for half in range(2):
                groups.append(([(fw1_in, 4 * half + m, k) for m in range(4)],
                               fw1_t[:, k, 512 * half:512 * half + 512], None, None))
        for k in range(0, KE, 2):
            groups.append(([(w2_in, e, k + i) for i in range(2) for e in range(KD)],
                           w2_hi[:, k:k + 2, :].rearrange("p k e -> p (k e)"),
                           w2_lo[:, k:k + 2, :].rearrange("p k e -> p (k e)"), 2))
        for k in range(KC):
            groups.append(([(w1_in, m, k) for m in range(KE)], w1_hi[:, k, :], w1_lo[:, k, :], 1))
        scaled_upto = [sum(g[2] is not None for g in groups[:n + 1]) for n in range(len(groups))]
        plain_upto = [sum(g[2] is None for g in groups[:n + 1]) for n in range(len(groups))]

        def group_out(eng, n):
            if groups[n][2] is not None:
                eng.wait_ge(p_lo, scaled_upto[n])
            else:
                eng.wait_ge(p_plain, plain_upto[n])

        def prepared(eng):
            eng.wait_ge(p_lo, scaled_upto[-1])
            eng.wait_ge(p_plain, plain_upto[-1])
            eng.wait_ge(p_scales, 3)
            eng.wait_ge(p_tab, 64)

        block = ctx.enter_context(nc.Block())

        @block.sync
        def _(sp):
            sp.dma_start(wo_in, w_omega.rearrange("(m p) d -> p m d", p=P)).then_inc(p_wo, 16)
            sp.dma_start(b_om[:, :], b_omega.rearrange("(m p) -> p m", p=P),
                         allow_slow_non_contiguous=True).then_inc(p_vec, 16)
            sp.dma_start(lscale[:, :], log_scale.rearrange("(m p) -> p m", p=P),
                         allow_slow_non_contiguous=True).then_inc(p_vec, 16)
            sp.dma_start(b1_raw[:, :], b1.rearrange("(m p) -> p m", p=P),
                         allow_slow_non_contiguous=True).then_inc(p_vec, 16)
            sp.dma_start(fb1[:, :], f_b1.rearrange("(m p) -> p m", p=P),
                         allow_slow_non_contiguous=True).then_inc(p_vec, 16)
            sp.dma_start(fw2_in, f_w2.rearrange("(m p) f -> p m f", p=P)).then_inc(p_fw2, 16)
            sp.dma_start(fw1_in, f_w1.rearrange("(m p) d -> p m d", p=P)).then_inc(p_fw1, 16)
            sp.dma_start(pos_rsqrt[:, :], pos_table[0].partition_broadcast(P)).then_inc(p_tab, 16)
            sp.dma_start(pos_inv[:, :], pos_table[1].partition_broadcast(P)).then_inc(p_tab, 16)
            sp.dma_start(b2_rows[:, :], b2.partition_broadcast(P)).then_inc(p_tab, 16)
            sp.dma_start(fb2_rows[:, :], f_b2.partition_broadcast(P)).then_inc(p_tab, 16)

            def step(s):
                if c := s.chunk(4):
                    need(sp, base_done, c, 2)
                    sp.dma_start(x_rows[:, c.b], x_v[c.index]).then_inc(x_loaded[c.b], 16)
                if c := s.chunk(0):
                    need(sp, out_done, c)
                    sp.dma_start(out_v[c.index], x1[:, c.b]).then_inc(stored[c.b], 16)

            run(sp, step, -4)
            for i in range(2):
                sp.wait_ge(stored[i], 16 * (CHUNKS // 2))

        @block.gpsimd
        def _(pool):
            pool.memset(ident[:, :], 0.0).then_inc(p_zero, 1)
            pool.wait_ge(p_zero, 1)
            pool.affine_select(out=ident[:, :], in_=ident[:, :], compare_op=ALU.not_equal, fill=1.0, base=0,
                               pattern=[[-1, P]], channel_multiplier=1).then_inc(p_ident, 1)
            pool.memset(e_base[:, :], 2.718281828459045).then_inc(p_const, 1)
            pool.memset(minus_half[:, :], -0.5).then_inc(p_const, 1)
            pool.wait_ge(p_const, 2)
            pool.wait_ge(p_vec, 64)
            pool.tensor_tensor(exp_ls[:, :], e_base[:, :], lscale[:, :], ALU.pow).then_inc(p_exp, 1)
            pool.wait_ge(p_mags, 5)
            pool.partition_all_reduce(mags_all[:, :], mags[:, :], P, ABSMAX).then_inc(p_max, 1)
            prepared(pool)

            def inverse_std_1(c):
                need(pool, ve1_done, c)
                pool.tensor_tensor(rs1[:, c.b], ve1[:, :], minus_half[:, :], ALU.pow).then_inc(rs1_done, 1)

            def residual_base(c):
                need(pool, scaled_done, c)
                pool.tensor_tensor(base[:, c.b], base[:, c.b], b2_rows[:, :].unsqueeze(1).to_broadcast([P, NT, D]),
                                   ALU.add).then_inc(base_done, 1)

            def inverse_std_2(c):
                need(pool, ve2_done, c)
                pool.tensor_tensor(rs2[:, :], ve2[:, :], minus_half[:, :], ALU.pow).then_inc(rs2_done, 1)

            def add_output_bias(c):
                need(pool, xs2_done, c)
                pool.tensor_tensor(x1[:, c.b], x1[:, c.b], fb2_rows[:, :].unsqueeze(1).to_broadcast([P, NT, D]),
                                   ALU.add).then_inc(xb_done, 1)

            def memory_imag(c):
                need(pool, sumi_done, c)
                need(pool, icarry_done, c)
                table = pos_inv[:, c.b * CH:(c.b + 1) * CH].unsqueeze(1).to_broadcast([P, KD, CH])
                pool.tensor_tensor(mi[:, :, :], mi[:, :, :], table, ALU.mult).then_inc(mi_done, 1)

            def product_real_sin(c):
                need(pool, mr_done, c)
                need(pool, sin_done, c)
                need(pool, ri_done, c, 1)
                pool.tensor_tensor(qb[:, :, :], mr[:, :, :], sn[:, :, :], ALU.mult).then_inc(qb_done, 1)

            def retrieve_imag(c):
                need(pool, rb_done, c)
                need(pool, qb_done, c)
                pool.tensor_tensor(ri[:, :, :], ri[:, :, :], qb[:, :, :], ALU.subtract).then_inc(ri_done, 1)

            def product_imag_sin(c):
                need(pool, mi_done, c)
                need(pool, sin_done, c)
                need(pool, rr_done, c, 1)
                pool.tensor_tensor(qa[:, :, :], mi[:, :, :], sn[:, :, :], ALU.mult).then_inc(qa_done, 1)

            def context_sums(c):
                need(pool, ch_done[0], c)
                need(pool, cl_done[0], c)
                need(pool, cmi_done, c)
                need(pool, sumr_done, c)
                pool.tensor_tensor(cmr[:, :, :], cmr[:, :, :], cmi[:, :, :], ALU.add).then_inc(s2_done, 1)
                need(pool, sqr_done, c)
                need(pool, sqi_done, c)
                pool.tensor_tensor(sqr[:, :, :], sqr[:, :, :], turn[:, :, :], ALU.add).then_inc(q2_done, 1)
                need(pool, s2_done, c)
                need(pool, rr_done, c)
                pool.tensor_tensor(cmr[:, :, :], cmr[:, :, :], rr[:, :, :], ALU.add).then_inc(s3_done, 1)
                need(pool, s3_done, c)
                need(pool, ri_done, c)
                pool.tensor_tensor(cmr[:, :, :], cmr[:, :, :], ri[:, :, :], ALU.add).then_inc(s4_done, 1)
                need(pool, q2_done, c)
                pool.tensor_tensor(sqr[:, 0], sqr[:, 0], sqr[:, 1], ALU.add).then_inc(q_done, 1)
                need(pool, s4_done, c)
                pool.tensor_tensor(cmr[:, 0], cmr[:, 0], cmr[:, 1], ALU.add).then_inc(s_done, 1)

            def inverse_std_context(c):
                need(pool, cve_done, c)
                pool.tensor_tensor(crs[:, :], cve[:, :], minus_half[:, :], ALU.pow).then_inc(crs_done, 1)

            def step(s):
                if c := s.chunk(0):
                    inverse_std_2(c)
                if c := s.chunk(1):
                    inverse_std_context(c)
                if c := s.chunk(3):
                    inverse_std_1(c)
                if c := s.chunk(0):
                    add_output_bias(c)
                if c := s.chunk(2):
                    residual_base(c)
                    memory_imag(c)
                    product_imag_sin(c)
                    product_real_sin(c)
                    retrieve_imag(c)
                    context_sums(c)

            run(pool, step, -3)

        @block.scalar
        def _(act):
            act.dma_start(gamma_rows, ln_gamma.partition_broadcast(P)).then_inc(p_w1, 16)
            act.dma_start(beta_rows, ln_beta.partition_broadcast(P)).then_inc(p_w1, 16)
            act.dma_start(w1_in, w1.rearrange("(m p) c -> p m c", p=P)).then_inc(p_w1, 16)
            act.dma_start(w2_in, w2.rearrange("(m p) f -> p m f", p=P)).then_inc(p_w2, 16)
            dump = base[:, :, :, :].rearrange("p b t d -> p (b t d)")
            for i, (s, w) in enumerate(((p_fw1, fw1_in), (p_fw2, fw2_in))):
                act.wait_ge(s, 16)
                if i:
                    act.wait_ge(p_abs, i)
                act.activation(dump, w.rearrange("p m d -> p (m d)"), ACT.Abs,
                               accum_out=abs_sums[:, i:i + 1]).then_inc(p_abs, 1)
            for n, (tiles, hi, lo, scale) in enumerate(groups):
                if lo is None:
                    act.wait_ge(p_turned, n + 1)
                    act.copy(hi, ps[:, n % 8, :]).then_inc(p_plain, 1)
                else:
                    act.wait_ge(p_turned, n + 1)
                    act.wait_ge(p_scales, 1)
                    act.activation(hi, ps[:, n % 8, :], ACT.Copy, scale=up[:, scale:scale + 1]).then_inc(p_hi, 1)
            prepared(act)

            def base_scaled(c):
                need(act, gain_done, c)
                need(act, x1_done, c, 2)
                for j in range(NT):
                    last = act.activation(base[:, c.b, j], x_rows[:, c.b, j], ACT.Identity,
                                          scale=gain1[:, c.b, j:j + 1], bias=shift1[:, c.b, j:j + 1])
                last.then_inc(scaled_done, 1)

            def omega_out(c):
                need(act, omega_done, c)
                need(act, abs_done, c, 1)
                need(act, sin_done, c, 1)
                for e in range(KD):
                    last = act.activation(ph[:, e], ps[:, 2 + e], ACT.Identity, scale=om_scale[:, e:e + 1],
                                          bias=om_bias[:, e:e + 1])
                last.then_inc(w_done, 1)

            def sin_cos(c):
                need(act, frac_done, c)
                act.activation(turn[:, :, :], ph[:, :, :], ACT.Abs).then_inc(abs_done, 1)
                need(act, ri_done, c, 1)
                need(act, qa_done, c, 1)
                act.activation(sn[:, :, :], ph[:, :, :], ACT.Sin, scale=TWO_PI).then_inc(sin_done, 1)
                need(act, abs_done, c)
                act.activation(cs[:, :, :], turn[:, :, :], ACT.Sin, scale=-TWO_PI,
                               bias=half_pi[:, 0:1]).then_inc(cos_done, 1)

            def context_hi(c, part, ready, src):
                need(act, ready, c)
                need(act, w1_done[KE - 1], c, 2)
                act.copy(ch[:, c.b, 2 * part:2 * part + 2], src).then_inc(ch_done[part], 1)

            def square_real(c):
                need(act, mr_done, c)
                need(act, stats_done, c, 1)
                act.activation(sqr[:, :, :], mr[:, :, :], ACT.Square).then_inc(sqr_done, 1)

            def square_imag(c):
                need(act, mi_done, c)
                need(act, cos_done, c)
                act.activation(turn[:, :, :], mi[:, :, :], ACT.Square).then_inc(sqi_done, 1)

            def spread_out(c):
                need(act, spread_done, c)
                need(act, z_done[KE - 1], c, 1)
                act.copy(rb[:, :], ps[:, 2]).then_inc(rbs_done, 1)

            def gelu(c, m):
                need(act, z_done[m], c)
                act.activation(z[:, m], z[:, m], ACT.Gelu, scale=down[:, 1:2], bias=b1_full[:, m:m + 1])\
                   .then_inc(g_done[m], 1)
                need(act, g_done[m], c)
                need(act, w2_done, c, 1)
                act.activation(gh[:, m], z[:, m], ACT.Copy, scale=up[:, 3:4]).then_inc(gh_done[m], 1)

            def second_hi(c):
                need(act, t2_done, c)
                need_block(act, f1_done, KF - 1, c, 1)
                act.copy(h2[:, :, :], ps[:, 0:2]).then_inc(h2_done, 1)

            def first_out(c):
                need(act, t1_done, c)
                need(act, cmr_done, c, 1)
                need(act, cmi_done, c, 1)
                act.copy(xf[:, :, :], ps[:, 2:4]).then_inc(xf_done, 1)
                need(act, xf_done, c)
                act.copy(xh[:, :, :], xf[:, :, :]).then_inc(xh_done, 1)

            def relu(c, m):
                need_block(act, f1_done, m, c)
                if m >= SLOTS:
                    need_block(act, rl_done, m - SLOTS, c)
                else:
                    need_block(act, rl_done, m + SLOTS, c, 1)
                act.activation(rf[:, m % SLOTS], ps[:, 6 + m % 2], ACT.Relu, scale=relu_scale[:, 0:1],
                               bias=relu_bias[:, m:m + 1]).then_inc(relu_done[m % SLOTS], 1)

            def relu_hi(c, m):
                need_block(act, relu_done, m, c)
                if m >= SLOTS:
                    need_block(act, f2_done, m - SLOTS, c)
                else:
                    need_block(act, f2_done, m + SLOTS, c, 1)
                act.copy(rh[:, m % SLOTS], rf[:, m % SLOTS]).then_inc(rh_done[m % SLOTS], 1)

            def step(s):
                now, nxt, ahead, far = s.chunk(0), s.chunk(1), s.chunk(2), s.chunk(3)
                if ahead:
                    omega_out(ahead)
                    sin_cos(ahead)
                    base_scaled(ahead)
                    context_hi(ahead, 0, cmr_done, cmr[:, :, :])
                    context_hi(ahead, 1, cmi_done, cmi[:, :, :])
                if now:
                    second_hi(now)
                if ahead:
                    square_real(ahead)
                if nxt:
                    spread_out(nxt)
                    gelu(nxt, 0)
                    gelu(nxt, 1)
                if nxt:
                    gelu(nxt, 2)
                for m in range(KF):
                    if now:
                        relu(now, m)
                        if m:
                            relu_hi(now, m - 1)
                    if m == 2 and ahead:
                        square_imag(ahead)
                    if m == 3 and nxt:
                        gelu(nxt, 3)
                    if m == 5 and far:
                        first_out(far)
                if now:
                    relu_hi(now, KF - 1)
                if ahead:
                    context_hi(ahead, 2, rr_done, rr[:, :, :])
                    context_hi(ahead, 3, ri_done, ri[:, :, :])

            run(act, step, -3)

        @block.tensor
        def _(pe):
            pe.wait_ge(p_ident, 1)
            pe.wait_ge(p_ones, 1)
            pe.wait_ge(p_abs, 2)
            pe.matmul(ps[:, 7, 0:2], ones[:, 0:P], abs_sums[:, :], start=True, stop=True).then_inc(p_mean, 1)
            for n, (tiles, hi, lo, scale) in enumerate(groups):
                if scale == 0:
                    pe.wait_ge(p_wo, 16)
                elif scale == 1:
                    pe.wait_ge(p_fold, 1)
                elif scale == 2:
                    pe.wait_ge(p_w2, 16)
                else:
                    pe.wait_ge(p_tern, 2)
                if n >= 8:
                    group_out(pe, n - 8)
                for q, (src, m, k) in enumerate(tiles):
                    last = pe.transpose(ps[:, n % 8, q * P:(q + 1) * P], src[:, m, k * P:(k + 1) * P], ident[:, :])
                last.then_inc(p_turned, 1)
            prepared(pe)

            def first_transposes(c):
                need(pe, xs_done, c)
                need(pe, rbs_done, c, 2)
                need(pe, csq_done, c, 2)
                for k in range(KD):
                    for j in range(NT):
                        last = pe.transpose(ps[:, 2 + k, j * P:(j + 1) * P], xs[:, j, k * P:(k + 1) * P], ident[:, :])
                last.then_inc(t1_done, 1)

            def omega(c):
                need(pe, xh_done, c)
                need(pe, xl_done, c)
                for e in range(KD):
                    passes = [(w, a, k) for w, a in ((wo_hi, xh), (wo_hi, xl), (wo_lo, xh)) for k in range(KD)]
                    for i, (w, a, k) in enumerate(passes):
                        last = pe.matmul(ps[:, 2 + e], w[:, k, e * P:(e + 1) * P], a[:, k],
                                         start=(i == 0), stop=(i == len(passes) - 1))
                last.then_inc(omega_done, 1)

            def context_stats(c, after):
                need(pe, s_done, c)
                need(pe, q_done, c)
                if after:
                    need(pe, w_done, after)
                for i, src in enumerate((cmr, sqr)):
                    for j in range(NT):
                        col = i * NT + j
                        last = pe.matmul(ps[:, 3, col:col + 1], src[:, 0, j * P:(j + 1) * P], ones[:, 0:1],
                                         start=True, stop=True)
                last.then_inc(stats_done, 1)

            def spread(c):
                need(pe, diag_done, c)
                pe.matmul(ps[:, 2], ones[:, 0:P], diag[:, :, :], start=True, stop=True).then_inc(spread_done, 1)

            def hidden(c, m):
                if m < 2:
                    need(pe, x1_done, c, 1)
                else:
                    need_block(pe, relu_done, KF - 4 + m, c, 2)
                if m == 0:
                    for part in range(4):
                        need(pe, ch_done[part], c)
                        need(pe, cl_done[part], c)
                passes = [(w, a, k) for k in range(KC) for w, a in ((w1_hi, ch), (w1_hi, cl), (w1_lo, ch))]
                for i, (w, a, k) in enumerate(passes):
                    last = pe.matmul(ps[:, 4 + m], w[:, k, m * P:(m + 1) * P], a[:, c.b, k],
                                     start=(i == 0), stop=(i == len(passes) - 1))
                last.then_inc(w1_done[m], 1)

            def second_transposes(c):
                need(pe, xs2_done, c)
                need(pe, out_done, c, 1)
                for k in range(KD):
                    for j in range(NT):
                        last = pe.transpose(ps[:, k, j * P:(j + 1) * P], xs2[:, j, k * P:(k + 1) * P], ident[:, :])
                last.then_inc(t2_done, 1)

            def ffn_in(c, m, after):
                if m == 0:
                    need(pe, h2_done, c)
                    need(pe, l2_done, c)
                if m >= 2:
                    need_block(pe, relu_done, m - 2, c)
                elif after:
                    need(pe, z_done[2 + m], after)
                passes = [(a, k) for k in range(KD) for a in (h2, l2)]
                for i, (a, k) in enumerate(passes):
                    last = pe.matmul(ps[:, 6 + m % 2], fw1_t[:, k, m * P:(m + 1) * P], a[:, k],
                                     start=(i == 0), stop=(i == len(passes) - 1))
                last.then_inc(f1_done[m % SLOTS], 1)

            def ffn_out(c, m):
                need_block(pe, rh_done, m, c)
                need_block(pe, rl_done, m, c)
                for j in range(NT):
                    for a in (rh, rl):
                        last = pe.matmul(ps_rows_a[:, j], a[:, m % SLOTS, j * P:(j + 1) * P], fw2_t[:, m],
                                         start=(m == 0 and j % 2 == 0 and a is rh), stop=(m == KF - 1 and a is rl),
                                         skip_group_check=True)
                last.then_inc(f2_done[m % SLOTS], 1)

            def mixer_out(c):
                for m in range(KE):
                    need(pe, gh_done[m], c)
                    need(pe, gl_done[m], c)
                for j in range(NT):
                    passes = [(a, w, m) for m in range(KE) for a, w in ((gh, w2_hi), (gh, w2_lo), (gl, w2_hi))]
                    for i, (a, w, m) in enumerate(passes):
                        last = pe.matmul(ps_rows_b[:, j], a[:, m, j * P:(j + 1) * P], w[:, m],
                                         start=(i == 0), stop=(i == len(passes) - 1))
                last.then_inc(w2_done, 1)

            def step(s):
                now, nxt, ahead, far = s.chunk(0), s.chunk(1), s.chunk(2), s.chunk(3)
                if ahead:
                    omega(ahead)
                if nxt:
                    hidden(nxt, 0)
                    context_stats(nxt, ahead)
                    hidden(nxt, 1)
                if now:
                    second_transposes(now)
                if nxt:
                    hidden(nxt, 2)
                    spread(nxt)
                    hidden(nxt, 3)
                for m in range(KF):
                    if now:
                        ffn_in(now, m, nxt)
                        if m >= LAG:
                            ffn_out(now, m - LAG)
                    if m == 1 and far:
                        first_transposes(far)
                if nxt:
                    mixer_out(nxt)
                if now:
                    for m in range(KF - LAG, KF):
                        ffn_out(now, m)

            run(pe, step, -3)

        @block.vector
        def _(dve):
            done = [0]

            def link(ins):
                done[0] += 1
                ins.then_inc(p_dve, 1)
                dve.wait_ge(p_dve, done[0])

            dve.memset(ones[:, :], 1.0).then_inc(p_ones, 1)
            link(dve.memset(half_pi[:, :], PI / 2))
            dve.wait_ge(p_wo, 16)
            dve.tensor_reduce(mags[:, 0:1], wo_in, AX.XY, ALU.max,
                              apply_absolute_value=True).then_inc(p_mags, 1)
            dve.wait_ge(p_vec, 64)
            dve.tensor_reduce(mags[:, 4:5], fb1[:, :], AX.X, ALU.max,
                              apply_absolute_value=True).then_inc(p_mags, 1)
            dve.wait_ge(p_w2, 16)
            dve.tensor_reduce(mags[:, 2:3], w2_in, AX.XY, ALU.max,
                              apply_absolute_value=True).then_inc(p_mags, 1)
            dve.wait_ge(p_w1, 48)
            for m in range(KE):
                link(dve.tensor_tensor_reduce(w_tmp[:, 0:C], w1_in[:, m], beta_rows, 1.0, 0.0, ALU.mult, ALU.add,
                                              b1_dot[:, m:m + 1]))
            link(dve.tensor_tensor(b1_full[:, :], b1_dot[:, :], b1_raw[:, :], ALU.add))
            dve.tensor_reduce(mags[:, 3:4], b1_full[:, :], AX.X, ALU.max,
                              apply_absolute_value=True).then_inc(p_mags, 1)
            link(dve.tensor_tensor(w1_in, w1_in, gamma_rows.unsqueeze(1).to_broadcast([P, KE, C]), ALU.mult))
            link(dve.tensor_reduce(row_mean[:, :], w1_in, AX.X, ALU.add))
            link(dve.tensor_scalar(row_mean[:, :], row_mean[:, :], 1.0 / C, None, ALU.mult))
            for m in range(KE):
                fold = dve.tensor_scalar(w1_in[:, m], w1_in[:, m], row_mean[:, m:m + 1], None, ALU.subtract)
            fold.then_inc(p_fold, 1)
            dve.wait_ge(p_fold, 1)
            dve.tensor_reduce(mags[:, 1:2], w1_in, AX.XY, ALU.max,
                              apply_absolute_value=True).then_inc(p_mags, 1)
            dve.wait_ge(p_mean, 1)
            link(dve.tensor_scalar(thr[:, :], ps[:, 7, 0:2], 1.0 / (F * D), EPS, ALU.mult, ALU.add))
            link(dve.tensor_scalar(neg_thr[:, :], thr[:, :], -0.5, None, ALU.mult))
            link(dve.tensor_scalar(thr[:, :], thr[:, :], 0.5, None, ALU.mult))
            for i, w in enumerate((fw1_in, fw2_in)):
                flat = w.rearrange("p m d -> p (m d)")
                link(dve.tensor_scalar(w_tmp, flat, neg_thr[:, i:i + 1], None, ALU.is_lt))
                dve.scalar_tensor_tensor(out=flat, in0=flat, scalar=thr[:, i:i + 1], in1=w_tmp, op0=ALU.is_gt,
                                         op1=ALU.subtract).then_inc(p_tern, 1)
                dve.wait_ge(p_tern, i + 1)
            dve.wait_ge(p_max, 1)
            link(dve.tensor_copy(pw[:, 0:3], mags_all[:, 0:3]))
            link(dve.scalar_tensor_tensor(out=pw[:, 3:4], in0=mags_all[:, 1:2], scalar=float(C),
                                          in1=mags_all[:, 3:4], op0=ALU.mult, op1=ALU.add))
            link(dve.tensor_scalar(pw[:, 4:5], mags_all[:, 4:5], float(D), None, ALU.add))
            link(dve.tensor_scalar(pw[:, :], pw[:, :], 1e-30, None, ALU.max))
            link(dve.tensor_scalar(pw[:, :].bitcast(U32), pw[:, :].bitcast(U32), EXPONENT_BITS, None,
                                   ALU.bitwise_and))
            link(dve.reciprocal(up[:, :], pw[:, :]))
            link(dve.tensor_scalar(up[:, :], up[:, :], 2.0 ** 14, None, ALU.mult))
            dve.tensor_scalar(down[:, :], pw[:, :], 2.0 ** -14, None, ALU.mult).then_inc(p_scales, 1)
            dve.wait_ge(p_scales, 1)
            dve.wait_ge(p_exp, 1)
            link(dve.tensor_scalar(om_scale[:, :], exp_ls[:, :], down[:, 0:1], 1.0 / (2 * PI * LN_SCALE),
                                   ALU.mult, ALU.mult))
            link(dve.tensor_tensor(om_bias[:, :], exp_ls[:, :], b_om[:, :], ALU.mult))
            link(dve.tensor_scalar(om_bias[:, :], om_bias[:, :], 1.0 / (2 * PI), None, ALU.mult))
            dve.tensor_tensor(h_down[:, :], down[:, 2:3], down[:, 3:4], ALU.mult).then_inc(p_scales, 1)
            link(dve.tensor_scalar(relu_scale[:, :], up[:, 4:5], 1.0 / LN_SCALE, None, ALU.mult))
            dve.tensor_scalar(relu_bias[:, :], fb1[:, :], up[:, 4:5], None, ALU.mult).then_inc(p_scales, 1)
            for n, (tiles, hi, lo, scale) in enumerate(groups):
                if lo is not None:
                    dve.wait_ge(p_hi, scaled_upto[n])
                    dve.scalar_tensor_tensor(out=lo, in0=ps[:, n % 8, :], scalar=up[:, scale:scale + 1], in1=hi,
                                             op0=ALU.mult, op1=ALU.subtract).then_inc(p_lo, 1)
            prepared(dve)

            def statistics_1(c):
                need_dma(dve, x_loaded, c)
                need(dve, mv1_done, c, 1)
                for j in range(NT):
                    last = dve.bn_stats(bn1[:, j], x_rows[:, c.b, j])
                last.then_inc(bn1_done, 1)
                stand_alone(dve)
                need(dve, bn1_done, c)
                need(dve, base_done, c, 2)
                for j in range(NT):
                    last = dve.bn_aggr(mv1[:, c.b, j], bn1[:, j])
                last.then_inc(mv1_done, 1)
                need(dve, mv1_done, c)
                need(dve, rs1_done, c, 1)
                dve.tensor_scalar(ve1[:, :], mv1[:, c.b, :, 1], EPS, LN_SCALE ** -2, ALU.add, ALU.mult)\
                   .then_inc(ve1_done, 1)

            def normalise_1(c):
                need(dve, t1_done, c, 1)
                need(dve, rs1_done, c)
                for j in range(NT):
                    last = dve.tensor_scalar(xs[:, j], x_rows[:, c.b, j], mv1[:, c.b, j, 0:1],
                                             rs1[:, c.b, j:j + 1], ALU.subtract, ALU.mult)
                last.then_inc(xs_done, 1)

            def normalise_2(c):
                need(dve, t2_done, c, 1)
                need(dve, rs2_done, c)
                for j in range(NT):
                    last = dve.tensor_scalar(xs2[:, j], x1[:, c.b, j], mv2[:, j, 0:1], rs2[:, j:j + 1],
                                             ALU.subtract, ALU.mult)
                last.then_inc(xs2_done, 1)

            def gains_1(c):
                need(dve, rs1_done, c)
                dve.tensor_scalar(gain1[:, c.b], rs1[:, c.b], 1.0 / LN_SCALE, 1.0, ALU.mult, ALU.add)
                dve.scalar_tensor_tensor(out=shift1[:, c.b], in0=rs1[:, c.b], scalar=-1.0 / LN_SCALE,
                                         in1=mv1[:, c.b, :, 0], op0=ALU.mult, op1=ALU.mult).then_inc(gain_done, 1)
                dve.scalar_tensor_tensor(out=sq1[:, c.b], in0=rs1[:, c.b], scalar=float(D),
                                         in1=mv1[:, c.b, :, 1], op0=ALU.mult, op1=ALU.mult).then_inc(sq1a_done, 1)
                need(dve, sq1a_done, c)
                dve.tensor_tensor(sq1[:, c.b], sq1[:, c.b], rs1[:, c.b], ALU.mult).then_inc(sq1_done, 1)

            def first_lo(c):
                need(dve, xh_done, c)
                need(dve, omega_done, c, 1)
                dve.tensor_tensor(xl[:, :, :], xf[:, :, :], xh[:, :, :], ALU.subtract).then_inc(xl_done, 1)

            def phase(c):
                need(dve, w_done, c)
                table = pos_rsqrt[:, c.b * CH:(c.b + 1) * CH].unsqueeze(1).to_broadcast([P, KD, CH])
                dve.tensor_tensor(ph[:, :, :], ph[:, :, :], table, ALU.mult).then_inc(u_done, 1)
                need(dve, u_done, c)
                need(dve, ycarry_done, c, 1)
                for k in range(KD):
                    last = dve.tensor_tensor_scan(ph[:, k], ones[:, 0:1].to_broadcast([P, CH]), ph[:, k],
                                                  ph_carry[:, k] if c.b else 0.0, ALU.mult, ALU.add)
                last.then_inc(y_done, 1)
                need(dve, y_done, c)
                dve.tensor_copy(ph_carry[:, :, :], ph[:, :, CH - 1:CH]).then_inc(ycarry_done, 1)
                need(dve, q2_done, c, 1)
                dve.tensor_scalar(turn[:, :, :], ph[:, :, :], ROUND, ROUND, ALU.add, ALU.subtract)\
                   .then_inc(turn_done, 1)
                need(dve, turn_done, c)
                need(dve, ycarry_done, c)
                dve.tensor_tensor(ph[:, :, :], ph[:, :, :], turn[:, :, :], ALU.subtract).then_inc(frac_done, 1)

            def modulate(c):
                need(dve, cos_done, c)
                need(dve, stats_done, c, 1)
                dve.tensor_tensor(cmr[:, :, :], xf[:, :, :], cs[:, :, :], ALU.mult).then_inc(cmr_done, 1)
                need(dve, s2_done, c, 1)
                dve.tensor_tensor(cmi[:, :, :], xf[:, :, :], sn[:, :, :], ALU.mult).then_inc(cmi_done, 1)

            def prefix_sums(c):
                need(dve, cmi_done, c)
                need(dve, sqi_done, c, 1)
                need(dve, rcarry_done, c, 1)
                need(dve, icarry_done, c, 1)
                for k in range(KD):
                    last = dve.tensor_tensor_scan(mi[:, k], ones[:, 0:1].to_broadcast([P, CH]), cmi[:, k],
                                                  mi_carry[:, k] if c.b else 0.0, ALU.mult, ALU.add)
                last.then_inc(sumi_done, 1)
                for k in range(KD):
                    last = dve.tensor_tensor_scan(mr[:, k], ones[:, 0:1].to_broadcast([P, CH]), cmr[:, k],
                                                  mr_carry[:, k] if c.b else 0.0, ALU.mult, ALU.add)
                last.then_inc(sumr_done, 1)
                need(dve, sumi_done, c)
                dve.tensor_copy(mi_carry[:, :, :], mi[:, :, CH - 1:CH]).then_inc(icarry_done, 1)
                need(dve, sumr_done, c)
                dve.tensor_copy(mr_carry[:, :, :], mr[:, :, CH - 1:CH]).then_inc(rcarry_done, 1)

            def memory_real(c):
                need(dve, rcarry_done, c)
                table = pos_inv[:, c.b * CH:(c.b + 1) * CH].unsqueeze(1).to_broadcast([P, KD, CH])
                dve.tensor_tensor(mr[:, :, :], mr[:, :, :], table, ALU.mult).then_inc(mr_done, 1)

            def retrieve_real_cos(c):
                need(dve, mr_done, c)
                need(dve, s3_done, c, 1)
                dve.tensor_tensor(rr[:, :, :], mr[:, :, :], cs[:, :, :], ALU.mult).then_inc(ra_done, 1)

            def retrieve_imag_cos(c):
                need(dve, mi_done, c)
                need(dve, s4_done, c, 1)
                dve.tensor_tensor(ri[:, :, :], mi[:, :, :], cs[:, :, :], ALU.mult).then_inc(rb_done, 1)

            def retrieve(c):
                need(dve, ra_done, c)
                need(dve, qa_done, c)
                dve.tensor_tensor(rr[:, :, :], rr[:, :, :], qa[:, :, :], ALU.add).then_inc(rr_done, 1)

            def context_lo(c, part, src):
                need(dve, ch_done[part], c)
                need(dve, w1_done[KE - 1], c, 2)
                dve.tensor_tensor(cl[:, c.b, 2 * part:2 * part + 2], src, ch[:, c.b, 2 * part:2 * part + 2],
                                  ALU.subtract).then_inc(cl_done[part], 1)

            def context_variance(c):
                need(dve, stats_done, c)
                dve.tensor_scalar(cmu[:, :], ps[:, 3, 0:NT], 1.0 / C, None, ALU.mult).then_inc(cmu_done, 1)
                need(dve, sq1_done, c)
                dve.tensor_tensor(csq[:, :], ps[:, 3, NT:2 * NT], sq1[:, c.b], ALU.add).then_inc(csq_done, 1)
                need(dve, cmu_done, c)
                dve.tensor_tensor(cmu2[:, :], cmu[:, :], cmu[:, :], ALU.mult).then_inc(cmu2_done, 1)
                need(dve, cmu2_done, c)
                need(dve, csq_done, c)
                dve.scalar_tensor_tensor(out=cvar[:, :], in0=csq[:, :], scalar=1.0 / C, in1=cmu2[:, :],
                                         op0=ALU.mult, op1=ALU.subtract).then_inc(cvar_done, 1)
                need(dve, cvar_done, c)
                need(dve, crs_done, c, 1)
                dve.tensor_scalar(cve[:, :], cvar[:, :], 0.0, EPS * LN_SCALE ** 2, ALU.max, ALU.add)\
                   .then_inc(cve_done, 1)

            def diagonal(c):
                need(dve, crs_done, c)
                need(dve, spread_done, c, 1)
                for j in range(NT):
                    last = dve.tensor_scalar(diag[:, j], ident[:, :], crs[:, j:j + 1], None, ALU.mult)
                last.then_inc(diag_done, 1)

            def scale_hidden(c, m):
                need(dve, w1_done[m], c)
                need(dve, rbs_done, c)
                need(dve, gl_done[m], c, 1)
                dve.tensor_tensor(z[:, m], ps[:, 4 + m], rb[:, :], ALU.mult).then_inc(z_done[m], 1)

            def gelu_lo(c, m):
                need(dve, gh_done[m], c)
                need(dve, w2_done, c, 1)
                dve.scalar_tensor_tensor(out=gl[:, m], in0=z[:, m], scalar=up[:, 3:4], in1=gh[:, m],
                                         op0=ALU.mult, op1=ALU.subtract).then_inc(gl_done[m], 1)

            def mixer_residual(c):
                need(dve, w2_done, c)
                need(dve, base_done, c)
                need_dma(dve, stored, c, 2)
                dve.scalar_tensor_tensor(out=x1[:, c.b], in0=ps_rows_b, scalar=h_down[:, 0:1], in1=base[:, c.b],
                                         op0=ALU.mult, op1=ALU.add).then_inc(x1_done, 1)

            def statistics_2(c):
                need(dve, x1_done, c)
                need(dve, xs2_done, c, 1)
                for j in range(NT):
                    last = dve.bn_stats(bn2[:, j], x1[:, c.b, j])
                last.then_inc(bn2_done, 1)
                stand_alone(dve)
                need(dve, bn2_done, c)
                for j in range(NT):
                    last = dve.bn_aggr(mv2[:, j], bn2[:, j])
                last.then_inc(mv2_done, 1)
                need(dve, mv2_done, c)
                need(dve, rs2_done, c, 1)
                dve.tensor_scalar(ve2[:, :], mv2[:, :, 1], EPS, LN_SCALE ** -2, ALU.add, ALU.mult)\
                   .then_inc(ve2_done, 1)

            def second_lo(c):
                need(dve, h2_done, c)
                need_block(dve, f1_done, KF - 1, c, 1)
                dve.tensor_tensor(l2[:, :, :], ps[:, 0:2], h2[:, :, :], ALU.subtract).then_inc(l2_done, 1)

            def relu_lo(c, m):
                need_block(dve, rh_done, m, c)
                if m >= SLOTS:
                    need_block(dve, f2_done, m - SLOTS, c)
                else:
                    need_block(dve, f2_done, m + SLOTS, c, 1)
                dve.tensor_tensor(rl[:, m % SLOTS], rf[:, m % SLOTS], rh[:, m % SLOTS], ALU.subtract)\
                   .then_inc(rl_done[m % SLOTS], 1)

            def output(c):
                need_block(dve, f2_done, KF - 1, c)
                need(dve, xb_done, c)
                dve.scalar_tensor_tensor(out=x1[:, c.b], in0=ps_rows_a, scalar=down[:, 4:5], in1=x1[:, c.b],
                                         op0=ALU.mult, op1=ALU.add).then_inc(out_done, 1)

            def step(s):
                now, nxt, ahead, far = s.chunk(0), s.chunk(1), s.chunk(2), s.chunk(3)
                if now:
                    mixer_residual(now)
                    statistics_2(now)
                if ahead:
                    phase(ahead)
                if now:
                    normalise_2(now)
                if nxt:
                    context_variance(nxt)
                if far:
                    statistics_1(far)
                if ahead:
                    modulate(ahead)
                if nxt:
                    diagonal(nxt)
                if ahead:
                    prefix_sums(ahead)
                    memory_real(ahead)
                if far:
                    normalise_1(far)
                    gains_1(far)
                if now:
                    second_lo(now)
                if nxt:
                    scale_hidden(nxt, 0)
                    scale_hidden(nxt, 1)
                    scale_hidden(nxt, 2)
                if ahead:
                    retrieve_real_cos(ahead)
                if nxt:
                    scale_hidden(nxt, 3)
                if ahead:
                    retrieve_imag_cos(ahead)
                if nxt:
                    gelu_lo(nxt, 0)
                    gelu_lo(nxt, 1)
                    gelu_lo(nxt, 2)
                for m in range(KF):
                    if now:
                        relu_lo(now, m)
                    if m == 0 and ahead:
                        context_lo(ahead, 0, cmr[:, :, :])
                    if m == 1 and ahead:
                        retrieve(ahead)
                    if m == 2 and ahead:
                        context_lo(ahead, 1, cmi[:, :, :])
                    if m == 3 and nxt:
                        gelu_lo(nxt, 3)
                    if m == 5 and far:
                        first_lo(far)
                if ahead:
                    context_lo(ahead, 2, rr[:, :, :])
                    context_lo(ahead, 3, ri[:, :, :])
                if now:
                    output(now)

            run(dve, step, -3)


_INS = ['L0_attn_x', 'L0_attn_W_omega', 'L0_attn_b_omega', 'L0_attn_log_scale', 'L0_attn_ln_gamma',
        'L0_attn_ln_beta', 'L0_attn_W1', 'L0_attn_b1', 'L0_attn_W2', 'L0_attn_b2',
        'L0_ffn_W1', 'L0_ffn_b1', 'L0_ffn_W2', 'L0_ffn_b2']


def kernel(**inputs):
    import numpy as np
    import concourse.bacc as bacc
    from concourse.bass_utils import run_bass_kernel_spmd

    nc = bacc.Bacc("TRN2", target_bir_lowering=False, num_devices=1)
    arrays, args = {}, []
    for name in _INS:
        a = np.ascontiguousarray(inputs[name])
        arrays[f"in_{name}"] = a
        args.append(nc.dram_tensor(f"in_{name}", a.shape, mybir.dt.from_np(a.dtype), kind="ExternalInput").ap())
    shape = inputs['L0_attn_x'].shape
    position = np.arange(1, shape[1] + 1, dtype=np.float32)
    table = np.stack([np.float32(1) / np.sqrt(position), np.float32(1) / position]).astype(np.float32)
    arrays["in_positions"] = table
    args.append(nc.dram_tensor("in_positions", table.shape, F32, kind="ExternalInput").ap())
    args.append(nc.dram_tensor("out_0", shape, F32, kind="ExternalOutput").ap())
    phase_mixer_layer(nc, *args)
    r = run_bass_kernel_spmd(nc, [arrays], core_ids=[0])
    return r.results[0]["out_0"]
```

```python
from contextlib import ExitStack

import concourse.bass as bass
from concourse import mybir

ALU = mybir.AluOpType
ACT = mybir.ActivationFunctionType
AX = mybir.AxisListType
F32 = mybir.dt.float32
F16 = mybir.dt.float16
U32 = mybir.dt.uint32
ABSMAX = bass.bass_isa.ReduceOp.absmax

P = 128
EPS = 1e-5
PI = 3.141592653589793
LN_SCALE = 512.0
SQUARE_SCALE = 1.0 / 64
RSTD_SCALE = 2.0 ** 14
ROUND = 12582912.0
TWO_PI = 6.283185
EXPONENT_BITS = 0x7F800000


def phase_mixer_layer(nc, x, w_omega, b_omega, log_scale, ln_gamma, ln_beta, w1, b1, w2, b2,
                      f_w1, f_b1, f_w2, f_b2, pos_table, out):
    BATCH, SEQ, D = x.shape
    E1, C = w1.shape
    F = f_w1.shape[0]
    CH = 512
    NT = CH // P
    CHUNKS = BATCH * SEQ // CH
    KD, KC, KE, KF = D // P, C // P, E1 // P, F // P
    PER_SEQ = SEQ // CH
    assert PER_SEQ == 2 and KD == 2 and C == 4 * D and KE == 4 and KF == 8
    SLOTS = 4
    LAG = 3
    LOOP_FROM, LOOP_TO = 2, CHUNKS - 4

    x_v = x.rearrange("b (c t p) d -> (b c) p t d", t=NT, p=P)
    out_v = out.rearrange("b (c t p) d -> (b c) p t d", t=NT, p=P)

    ctx = ExitStack()
    with ctx:
        def sb(name, shape, dt=F32):
            return ctx.enter_context(nc.sbuf_tensor(name, shape, dt))

        def sem(name):
            return ctx.enter_context(nc.semaphore(name))

        ident = sb("ident", [P, P])
        ones = sb("ones", [P, P])
        pos_rsqrt = sb("pos_rsqrt", [P, SEQ])
        pos_inv = sb("pos_inv", [P, SEQ])
        b2_rows = sb("b2_rows", [P, D])
        fb2_rows = sb("fb2_rows", [P, D])
        wo_hi = sb("wo_hi", [P, KD, D], F16)
        wo_lo = sb("wo_lo", [P, KD, D], F16)
        w1_hi = sb("w1_hi", [P, KC, E1], F16)
        w1_lo = sb("w1_lo", [P, KC, E1], F16)
        w2_hi = sb("w2_hi", [P, KE, D], F16)
        w2_lo = sb("w2_lo", [P, KE, D], F16)
        fw1_t = sb("fw1_t", [P, KD, F], F16)
        fw2_t = sb("fw2_t", [P, KF, D], F16)
        b_om = sb("b_om", [P, KD])
        lscale = sb("lscale", [P, KD])
        e_base = sb("e_base", [P, KD])
        exp_ls = sb("exp_ls", [P, KD])
        om_scale = sb("om_scale", [P, KD])
        om_bias = sb("om_bias", [P, KD])
        row_squares = sb("row_squares", [P, KE])
        one_half = sb("one_half", [P, 1])
        minus_mean = sb("minus_mean", [P, KE])
        b1_raw = sb("b1_raw", [P, KE])
        b1_dot = sb("b1_dot", [P, KE])
        b1_full = sb("b1_full", [P, KE])
        row_mean = sb("row_mean", [P, KE])
        fb1 = sb("fb1", [P, KF])
        relu_bias = sb("relu_bias", [P, KF])
        half_pi = sb("half_pi", [P, 1])
        minus_half = sb("minus_half", [P, NT])
        mags = sb("mags", [P, 5])
        mags_all = sb("mags_all", [P, 5])
        pw = sb("pw", [P, 5])
        up = sb("up", [P, 5])
        down = sb("down", [P, 5])
        h_down = sb("h_down", [P, 1])
        z_down = sb("z_down", [P, 1])
        relu_scale = sb("relu_scale", [P, 1])
        abs_sums = sb("abs_sums", [P, 2])
        thr = sb("thr", [P, 2])
        neg_thr = sb("neg_thr", [P, 2])

        x_rows = sb("x_rows", [P, 2, NT, D])
        base = sb("base", [P, 2, NT, D])
        x1 = sb("x1", [P, 2, NT, D])
        xs = sb("xs", [P, NT, D])
        xs2 = sb("xs2", [P, NT, D])
        bn1 = sb("bn1", [P, NT, 6])
        mv1 = sb("mv1", [P, 2, NT, 2])
        ve1 = sb("ve1", [P, NT])
        rs1 = sb("rs1", [P, 2, NT])
        gain1 = sb("gain1", [P, 2, NT])
        shift1 = sb("shift1", [P, 2, NT])
        sq1 = sb("sq1", [P, 2, NT])
        bn2 = sb("bn2", [P, NT, 6])
        mv2 = sb("mv2", [P, NT, 2])
        ve2 = sb("ve2", [P, NT])
        rs2 = sb("rs2", [P, NT])
        cmu = sb("cmu", [P, NT])
        cmu2 = sb("cmu2", [P, NT])
        csq = sb("csq", [P, NT])
        cvar = sb("cvar", [P, NT])
        cve = sb("cve", [P, NT])
        crs = sb("crs", [P, NT])
        diag_hi = sb("diag_hi", [P, NT, P], F16)
        diag_lo = sb("diag_lo", [P, NT, P], F16)

        xf = sb("xf", [P, KD, CH])
        xh = sb("xh", [P, KD, CH], F16)
        xl = sb("xl", [P, KD, CH], F16)
        ph = sb("ph", [P, KD, CH])
        ph_carry = sb("ph_carry", [P, KD, 1])
        turn = sb("turn", [P, KD, CH])
        sn = sb("sn", [P, KD, CH])
        cs = sb("cs", [P, KD, CH])
        cmr = sb("cmr", [P, KD, CH])
        cmi = sb("cmi", [P, KD, CH])
        mr = sb("mr", [P, KD, CH])
        mi = sb("mi", [P, KD, CH])
        mr_carry = sb("mr_carry", [P, KD, 1])
        mi_carry = sb("mi_carry", [P, KD, 1])
        rr = sb("rr", [P, KD, CH])
        ri = sb("ri", [P, KD, CH])
        qa = sb("qa", [P, KD, CH])
        qb = sb("qb", [P, KD, CH])
        sqr = sb("sqr", [P, KD, CH])
        rb = sb("rb", [P, CH])
        s_hi = cmr[:, 1, 0:CH // 2].bitcast(F16)
        s_lo = cmr[:, 1, CH // 2:CH].bitcast(F16)
        q_hi = sqr[:, 1, 0:CH // 2].bitcast(F16)
        q_lo = sqr[:, 1, CH // 2:CH].bitcast(F16)
        ones_h = sb("ones_h", [P, P], F16)
        h2 = sb("h2", [P, KD, CH], F16)
        l2 = sb("l2", [P, KD, CH], F16)
        rh = sb("rh", [P, SLOTS, CH], F16)
        rl = sb("rl", [P, SLOTS, CH], F16)
        KB = 256
        arena = sb("arena", [P, 56 * KB])
        ch = arena[:, 0:16 * KB].bitcast(F16).rearrange("p (b k n) -> p b k n", b=2, k=KC)
        cl = arena[:, 16 * KB:32 * KB].bitcast(F16).rearrange("p (b k n) -> p b k n", b=2, k=KC)
        z = arena[:, 32 * KB:40 * KB].rearrange("p (k n) -> p k n", k=KE)
        gh = arena[:, 40 * KB:44 * KB].bitcast(F16).rearrange("p (k n) -> p k n", k=KE)
        gl = arena[:, 44 * KB:48 * KB].bitcast(F16).rearrange("p (k n) -> p k n", k=KE)
        rf = arena[:, 48 * KB:56 * KB].rearrange("p (k n) -> p k n", k=SLOTS)
        w1_in = arena[:, 32 * KB:48 * KB].rearrange("p (m c) -> p m c", m=KE)
        gamma_rows = arena[:, 16 * KB:20 * KB]
        beta_rows = arena[:, 20 * KB:24 * KB]
        w_tmp = arena[:, 24 * KB:32 * KB]
        fw1_in = arena[:, 0:8 * KB].rearrange("p (m d) -> p m d", m=KF)
        fw2_in = arena[:, 8 * KB:16 * KB].rearrange("p (m f) -> p m f", m=KD)
        w2_in = arena[:, 48 * KB:52 * KB].rearrange("p (m f) -> p m f", m=KD)
        wo_in = arena[:, 52 * KB:54 * KB].rearrange("p (m d) -> p m d", m=KD)

        ps = ctx.enter_context(nc.psum_tensor("ps", [P, 8, CH], F32))
        ps_rows_a = ps[:, 0:2, :].rearrange("p b (t d) -> p (b t) d", d=D)
        ps_rows_b = ps[:, 4:6, :].rearrange("p b (t d) -> p (b t) d", d=D)

        p_vec = sem("p_vec")
        p_om = sem("p_om")
        p_pos = sem("p_pos")
        p_tab = sem("p_tab")
        p_wo = sem("p_wo")
        p_w1 = sem("p_w1")
        p_w2 = sem("p_w2")
        p_fw1 = sem("p_fw1")
        p_fw2 = sem("p_fw2")
        p_zero = sem("p_zero")
        p_ident = sem("p_ident")
        p_const = sem("p_const")
        p_ones = sem("p_ones")
        p_exp = sem("p_exp")
        p_abs = sem("p_abs")
        p_mean = sem("p_mean")
        p_dot = sem("p_dot")
        p_squares = sem("p_squares")
        p_gamma = sem("p_gamma")
        p_rows = sem("p_rows")
        p_dve = sem("p_dve")
        p_fold = sem("p_fold")
        p_mags = sem("p_mags")
        p_max = sem("p_max")
        p_scales = sem("p_scales")
        p_tern = sem("p_tern")
        p_turned = sem("p_turned")
        p_hi = sem("p_hi")
        p_lo = sem("p_lo")
        p_plain = sem("p_plain")

        x_loaded = [sem(f"x_loaded{i}") for i in range(2)]
        stored = [sem(f"stored{i}") for i in range(2)]
        bn1_done, mv1_done, ve1_done = sem("bn1_done"), sem("mv1_done"), sem("ve1_done")
        rs1_done, xs_done, gain_done = sem("rs1_done"), sem("xs_done"), sem("gain_done")
        sq1a_done, sq1_done = sem("sq1a_done"), sem("sq1_done")
        scaled_done, base_done = sem("scaled_done"), sem("base_done")
        t1_done, xf_done, xh_done, xl_done = sem("t1_done"), sem("xf_done"), sem("xh_done"), sem("xl_done")
        omega_done, w_done, u_done, y_done = sem("omega_done"), sem("w_done"), sem("u_done"), sem("y_done")
        ycarry_done, turn_done, frac_done = sem("ycarry_done"), sem("turn_done"), sem("frac_done")
        abs_done, sin_done, cos_done = sem("abs_done"), sem("sin_done"), sem("cos_done")
        cmr_done, cmi_done = sem("cmr_done"), sem("cmi_done")
        sumr_done, sumi_done = sem("sumr_done"), sem("sumi_done")
        rcarry_done, icarry_done = sem("rcarry_done"), sem("icarry_done")
        mr_done, mi_done = sem("mr_done"), sem("mi_done")
        qa_done, qb_done, ra_done, rb_done = sem("qa_done"), sem("qb_done"), sem("ra_done"), sem("rb_done")
        rr_done, ri_done = sem("rr_done"), sem("ri_done")
        ch_done = [sem(f"ch_done{i}") for i in range(4)]
        cl_done = [sem(f"cl_done{i}") for i in range(4)]
        sqr_done, sqi_done, q2_done, q_done = sem("sqr_done"), sem("sqi_done"), sem("q2_done"), sem("q_done")
        s2_done, s3_done, s4_done, s_done = sem("s2_done"), sem("s3_done"), sem("s4_done"), sem("s_done")
        qh_done, ql_done, sh_done, sl_done = sem("qh_done"), sem("ql_done"), sem("sh_done"), sem("sl_done")
        stats_done, cmu_done, cmu2_done = sem("stats_done"), sem("cmu_done"), sem("cmu2_done")
        csq_done, cvar_done, cve_done, crs_done = sem("csq_done"), sem("cvar_done"), sem("cve_done"), sem("crs_done")
        diag_hi_done = sem("diag_hi_done")
        diag_done, spread_done, rbs_done = sem("diag_done"), sem("spread_done"), sem("rbs_done")
        w1_done = [sem(f"w1_done{m}") for m in range(KE)]
        z_done = [sem(f"z_done{m}") for m in range(KE)]
        g_done = [sem(f"g_done{m}") for m in range(KE)]
        gh_done = [sem(f"gh_done{m}") for m in range(KE)]
        gl_done = [sem(f"gl_done{m}") for m in range(KE)]
        w2_done, x1_done = sem("w2_done"), sem("x1_done")
        bn2_done, mv2_done, ve2_done = sem("bn2_done"), sem("mv2_done"), sem("ve2_done")
        rs2_done, xs2_done, xb_done = sem("rs2_done"), sem("xs2_done"), sem("xb_done")
        t2_done, h2_done, l2_done = sem("t2_done"), sem("h2_done"), sem("l2_done")
        f1_done = [sem(f"f1_done{m}") for m in range(SLOTS)]
        relu_done = [sem(f"relu_done{m}") for m in range(SLOTS)]
        rh_done = [sem(f"rh_done{m}") for m in range(SLOTS)]
        rl_done = [sem(f"rl_done{m}") for m in range(SLOTS)]
        f2_done = [sem(f"f2_done{m}") for m in range(SLOTS)]
        out_done = sem("out_done")

        class Counts:
            def __init__(self, eng, even):
                self.eng, self.even, self.held = eng, even, {}
                if not isinstance(even, int):
                    for plus in range(7):
                        self.value(1, plus)
                    for plus in (0, 16, 32, 48):
                        self.value(8, plus)

            def value(self, times, plus):
                if isinstance(self.even, int):
                    return times * self.even + plus
                if (times, plus) not in self.held:
                    self.held[times, plus] = self.eng.snap(self.eng.to_reg(self.even * times + plus))
                return self.held[times, plus]

        class Step:
            def __init__(self, counts, odd):
                self.counts, self.odd = counts, odd

            def chunk(self, ahead):
                c = Chunk(self.counts, self.odd + ahead)
                return c if c.exists() else None

        class Chunk:
            def __init__(self, counts, more):
                self.counts, self.more = counts, more
                self.index = counts.even + more
                self.b = more % 2

            def exists(self):
                return not isinstance(self.index, int) or 0 <= self.index < CHUNKS

        def wait(eng, s, value):
            if not isinstance(value, int) or value > 0:
                eng.wait_ge(s, value)

        def need(eng, s, c, back=0):
            wait(eng, s, c.counts.value(1, c.more + 1 - back))

        def need_dma(eng, pair, c, back=0):
            wait(eng, pair[c.b], c.counts.value(8, 8 * (c.more - c.b - back) + 16))

        def need_block(eng, sems, m, c, back=0):
            wait(eng, sems[m % SLOTS], c.counts.value(2, 2 * (c.more - back) + m // SLOTS + 1))

        def stand_alone(eng):
            eng.wait_ge(p_ones, 1)

        def run(eng, step, first):
            for s in range(first, LOOP_FROM):
                step(Step(Counts(eng, s - s % 2), s % 2))
            with eng.Fori(LOOP_FROM // 2, LOOP_TO // 2) as pair:
                counts = Counts(eng, pair * 2)
                step(Step(counts, 0))
                step(Step(counts, 1))
            for s in range(LOOP_TO, CHUNKS):
                step(Step(Counts(eng, s - s % 2), s % 2))

        groups = [([(wo_in, e, k) for k in range(KD) for e in range(KD)],
                   wo_hi[:, :, :].rearrange("p k e -> p (k e)"), wo_lo[:, :, :].rearrange("p k e -> p (k e)"), 0)]
        for k in range(0, KF, 2):
            groups.append(([(fw2_in, m, k + i) for i in range(2) for m in range(KD)],
                           fw2_t[:, k:k + 2, :].rearrange("p k e -> p (k e)"), None, None))
        for k in range(KD):
            for half in range(2):
                groups.append(([(fw1_in, 4 * half + m, k) for m in range(4)],
                               fw1_t[:, k, 512 * half:512 * half + 512], None, None))
        for k in range(0, KE, 2):
            groups.append(([(w2_in, e, k + i) for i in range(2) for e in range(KD)],
                           w2_hi[:, k:k + 2, :].rearrange("p k e -> p (k e)"),
                           w2_lo[:, k:k + 2, :].rearrange("p k e -> p (k e)"), 2))
        for k in range(KC):
            groups.append(([(w1_in, m, k) for m in range(KE)], w1_hi[:, k, :], w1_lo[:, k, :], 1))
        scaled_upto = [sum(g[2] is not None for g in groups[:n + 1]) for n in range(len(groups))]
        plain_upto = [sum(g[2] is None for g in groups[:n + 1]) for n in range(len(groups))]

        group_banks = [(0, 1, 4, 5, 6, 7)[n % 6] for n in range(len(groups))]

        def group_out(eng, n):
            if groups[n][2] is not None:
                eng.wait_ge(p_lo, scaled_upto[n])
            else:
                eng.wait_ge(p_plain, plain_upto[n])

        def first_chunks(eng):
            return [Chunk(Counts(eng, 0), more) for more in range(2)]

        def prepared(eng):
            eng.wait_ge(p_lo, scaled_upto[-1])
            eng.wait_ge(p_plain, plain_upto[-1])
            eng.wait_ge(p_scales, 3)
            eng.wait_ge(p_tab, 48)

        block = ctx.enter_context(nc.Block())

        @block.sync
        def _(sp):
            sp.dma_start(wo_in, w_omega.rearrange("(m p) d -> p m d", p=P)).then_inc(p_wo, 16)
            sp.dma_start(x_rows[:, 0], x_v[0]).then_inc(x_loaded[0], 16)
            for vector, src in ((b1_raw, b1), (fb1, f_b1)):
                sp.dma_start(vector[:, :], src.rearrange("(m p) -> p m", p=P),
                             allow_slow_non_contiguous=True).then_inc(p_vec, 16)
            sp.dma_start(fw1_in, f_w1.rearrange("(m p) d -> p m d", p=P)).then_inc(p_fw1, 16)
            sp.dma_start(fw2_in, f_w2.rearrange("(m p) f -> p m f", p=P)).then_inc(p_fw2, 16)
            sp.dma_start(pos_rsqrt[:, :], pos_table[0].partition_broadcast(P)).then_inc(p_pos, 16)
            sp.dma_start(x_rows[:, 1], x_v[1]).then_inc(x_loaded[1], 16)
            sp.dma_start(pos_inv[:, :], pos_table[1].partition_broadcast(P)).then_inc(p_tab, 16)
            sp.dma_start(b2_rows[:, :], b2.partition_broadcast(P)).then_inc(p_tab, 16)
            sp.dma_start(fb2_rows[:, :], f_b2.partition_broadcast(P)).then_inc(p_tab, 16)

            def step(s):
                if c := s.chunk(4):
                    need(sp, base_done, c, 2)
                    sp.dma_start(x_rows[:, c.b], x_v[c.index]).then_inc(x_loaded[c.b], 16)
                if c := s.chunk(0):
                    need(sp, out_done, c)
                    sp.dma_start(out_v[c.index], x1[:, c.b]).then_inc(stored[c.b], 16)

            run(sp, step, -2)
            for i in range(2):
                sp.wait_ge(stored[i], 16 * (CHUNKS // 2))

        @block.gpsimd
        def _(pool):
            pool.memset(ident[:, :], 0.0).then_inc(p_zero, 1)
            pool.wait_ge(p_zero, 1)
            pool.affine_select(out=ident[:, :], in_=ident[:, :], compare_op=ALU.not_equal, fill=1.0, base=0,
                               pattern=[[-1, P]], channel_multiplier=1).then_inc(p_ident, 1)
            pool.memset(e_base[:, :], 2.718281828459045).then_inc(p_const, 1)
            pool.memset(minus_half[:, :], -0.5).then_inc(p_const, 1)
            pool.memset(one_half[:, :], 0.5).then_inc(p_const, 1)
            pool.wait_ge(p_const, 3)
            def inverse_std_1(c):
                need(pool, ve1_done, c)
                pool.tensor_tensor(rs1[:, c.b], ve1[:, :], minus_half[:, :], ALU.pow).then_inc(rs1_done, 1)

            def residual_base(c):
                need(pool, scaled_done, c)
                pool.tensor_tensor(base[:, c.b], base[:, c.b], b2_rows[:, :].unsqueeze(1).to_broadcast([P, NT, D]),
                                   ALU.add).then_inc(base_done, 1)

            def inverse_std_2(c):
                need(pool, ve2_done, c)
                pool.tensor_tensor(rs2[:, :], ve2[:, :], minus_half[:, :], ALU.pow).then_inc(rs2_done, 1)

            def add_output_bias(c):
                need(pool, xs2_done, c)
                pool.tensor_tensor(x1[:, c.b], x1[:, c.b], fb2_rows[:, :].unsqueeze(1).to_broadcast([P, NT, D]),
                                   ALU.add).then_inc(xb_done, 1)

            def memory_imag(c):
                need(pool, sumi_done, c)
                need(pool, icarry_done, c)
                table = pos_inv[:, c.b * CH:(c.b + 1) * CH].unsqueeze(1).to_broadcast([P, KD, CH])
                pool.tensor_tensor(mi[:, :, :], mi[:, :, :], table, ALU.mult).then_inc(mi_done, 1)

            def product_real_sin(c):
                need(pool, mr_done, c)
                need(pool, sin_done, c)
                need(pool, ri_done, c, 1)
                pool.tensor_tensor(qb[:, :, :], mr[:, :, :], sn[:, :, :], ALU.mult).then_inc(qb_done, 1)

            def retrieve_imag(c):
                need(pool, rb_done, c)
                need(pool, qb_done, c)
                pool.tensor_tensor(ri[:, :, :], ri[:, :, :], qb[:, :, :], ALU.subtract).then_inc(ri_done, 1)

            def product_imag_sin(c):
                need(pool, mi_done, c)
                need(pool, sin_done, c)
                need(pool, rr_done, c, 1)
                pool.tensor_tensor(qa[:, :, :], mi[:, :, :], sn[:, :, :], ALU.mult).then_inc(qa_done, 1)

            def context_sums(c):
                need(pool, ch_done[0], c)
                need(pool, cl_done[0], c)
                need(pool, cmi_done, c)
                need(pool, sumr_done, c)
                pool.tensor_tensor(cmr[:, :, :], cmr[:, :, :], cmi[:, :, :], ALU.add).then_inc(s2_done, 1)
                need(pool, s2_done, c)
                need(pool, rr_done, c)
                pool.tensor_tensor(cmr[:, :, :], cmr[:, :, :], rr[:, :, :], ALU.add).then_inc(s3_done, 1)
                need(pool, s3_done, c)
                need(pool, ri_done, c)
                pool.tensor_tensor(cmr[:, :, :], cmr[:, :, :], ri[:, :, :], ALU.add).then_inc(s4_done, 1)
                need(pool, sqr_done, c)
                need(pool, sqi_done, c)
                pool.tensor_tensor(sqr[:, :, :], sqr[:, :, :], turn[:, :, :], ALU.add).then_inc(q2_done, 1)
                need(pool, q2_done, c)
                pool.tensor_tensor(sqr[:, 0], sqr[:, 0], sqr[:, 1], ALU.add).then_inc(q_done, 1)
                need(pool, s4_done, c)
                pool.tensor_tensor(cmr[:, 0], cmr[:, 0], cmr[:, 1], ALU.add).then_inc(s_done, 1)

            def sums_lo(c):
                need(pool, q_done, c)
                need(pool, qh_done, c)
                pool.tensor_tensor(q_lo, sqr[:, 0], q_hi, ALU.subtract).then_inc(ql_done, 1)
                need(pool, s_done, c)
                need(pool, sh_done, c)
                pool.tensor_tensor(s_lo, cmr[:, 0], s_hi, ALU.subtract).then_inc(sl_done, 1)

            def inverse_std_context(c):
                need(pool, cve_done, c)
                pool.tensor_tensor(crs[:, :], cve[:, :], minus_half[:, :], ALU.pow).then_inc(crs_done, 1)
                need(pool, crs_done, c)
                need(pool, spread_done, c, 1)
                pool.tensor_tensor(diag_hi[:, :, :], ident[:, :].unsqueeze(1).to_broadcast([P, NT, P]),
                                   crs[:, :].unsqueeze(2).to_broadcast([P, NT, P]),
                                   ALU.mult).then_inc(diag_hi_done, 1)

            def step(s):
                if c := s.chunk(0):
                    inverse_std_2(c)
                if c := s.chunk(1):
                    inverse_std_context(c)
                if c := s.chunk(3):
                    inverse_std_1(c)
                if c := s.chunk(0):
                    add_output_bias(c)
                if c := s.chunk(2):
                    residual_base(c)
                    memory_imag(c)
                    product_imag_sin(c)
                    product_real_sin(c)
                    retrieve_imag(c)
                    context_sums(c)
                    sums_lo(c)

            first, second = first_chunks(pool)
            pool.wait_ge(p_mags, 1)
            pool.partition_all_reduce(mags_all[:, 0:1], mags[:, 0:1], P, ABSMAX).then_inc(p_max, 1)
            inverse_std_1(first)
            pool.wait_ge(p_om, 32)
            pool.tensor_tensor(exp_ls[:, :], e_base[:, :], lscale[:, :], ALU.pow).then_inc(p_exp, 1)
            for m in range(KE):
                pool.wait_ge(p_dot, m + 1)
                pool.tensor_tensor(w1_in[:, m], w1_in[:, m], gamma_rows, ALU.mult).then_inc(p_gamma, 1)
            inverse_std_1(second)
            pool.wait_ge(p_mags, 5)
            pool.partition_all_reduce(mags_all[:, 1:5], mags[:, 1:5], P, ABSMAX).then_inc(p_max, 1)
            pool.wait_ge(p_max, 2)
            pool.tensor_tensor(mags_all[:, 1:2], mags_all[:, 1:2], one_half[:, :], ALU.pow).then_inc(p_max, 1)
            pool.wait_ge(p_tab, 48)
            memory_imag(first)
            product_imag_sin(first)
            product_real_sin(first)
            retrieve_imag(first)
            residual_base(first)
            context_sums(first)
            sums_lo(first)
            prepared(pool)
            run(pool, step, -1)

        @block.scalar
        def _(act):
            for vector, src in ((b_om, b_omega), (lscale, log_scale)):
                act.dma_start(vector[:, :], src.rearrange("(m p) -> p m", p=P),
                              allow_slow_non_contiguous=True).then_inc(p_om, 16)
            act.dma_start(gamma_rows, ln_gamma.partition_broadcast(P)).then_inc(p_w1, 16)
            act.dma_start(beta_rows, ln_beta.partition_broadcast(P)).then_inc(p_w1, 16)
            act.dma_start(w1_in, w1.rearrange("(m p) c -> p m c", p=P)).then_inc(p_w1, 16)
            act.dma_start(w2_in, w2.rearrange("(m p) f -> p m f", p=P)).then_inc(p_w2, 16)
            def base_scaled(c):
                need(act, gain_done, c)
                need(act, x1_done, c, 2)
                for j in range(NT):
                    last = act.activation(base[:, c.b, j], x_rows[:, c.b, j], ACT.Identity,
                                          scale=gain1[:, c.b, j:j + 1], bias=shift1[:, c.b, j:j + 1])
                last.then_inc(scaled_done, 1)

            def omega_out(c):
                need(act, omega_done, c)
                need(act, abs_done, c, 1)
                need(act, sin_done, c, 1)
                for e in range(KD):
                    last = act.activation(ph[:, e], ps[:, 2 + e], ACT.Identity, scale=om_scale[:, e:e + 1],
                                          bias=om_bias[:, e:e + 1])
                last.then_inc(w_done, 1)

            def sin_cos(c):
                need(act, frac_done, c)
                act.activation(turn[:, :, :], ph[:, :, :], ACT.Abs).then_inc(abs_done, 1)
                need(act, ri_done, c, 1)
                need(act, qa_done, c, 1)
                act.activation(sn[:, :, :], ph[:, :, :], ACT.Sin, scale=TWO_PI).then_inc(sin_done, 1)
                need(act, abs_done, c)
                act.activation(cs[:, :, :], turn[:, :, :], ACT.Sin, scale=-TWO_PI,
                               bias=half_pi[:, 0:1]).then_inc(cos_done, 1)

            def context_hi(c, part, ready, src):
                need(act, ready, c)
                need(act, w1_done[KE - 1], c, 2)
                act.copy(ch[:, c.b, 2 * part:2 * part + 2], src).then_inc(ch_done[part], 1)

            def square_real(c):
                need(act, mr_done, c)
                need(act, stats_done, c, 1)
                act.activation(sqr[:, :, :], mr[:, :, :], ACT.Square, scale=SQUARE_SCALE).then_inc(sqr_done, 1)

            def sums_hi(c):
                need(act, q_done, c)
                act.copy(q_hi, sqr[:, 0]).then_inc(qh_done, 1)
                need(act, s_done, c)
                act.copy(s_hi, cmr[:, 0]).then_inc(sh_done, 1)

            def square_imag(c):
                need(act, mi_done, c)
                need(act, cos_done, c)
                act.activation(turn[:, :, :], mi[:, :, :], ACT.Square, scale=SQUARE_SCALE).then_inc(sqi_done, 1)

            def spread_out(c):
                need(act, spread_done, c)
                need(act, z_done[KE - 1], c, 1)
                act.copy(rb[:, :], ps[:, 2]).then_inc(rbs_done, 1)

            def gelu(c, m):
                need(act, z_done[m], c)
                act.activation(z[:, m], z[:, m], ACT.Gelu, scale=z_down[:, 0:1], bias=b1_full[:, m:m + 1])\
                   .then_inc(g_done[m], 1)
                need(act, g_done[m], c)
                need(act, w2_done, c, 1)
                act.activation(gh[:, m], z[:, m], ACT.Copy, scale=up[:, 3:4]).then_inc(gh_done[m], 1)

            def second_hi(c):
                need(act, t2_done, c)
                need_block(act, f1_done, KF - 1, c, 1)
                act.copy(h2[:, :, :], ps[:, 0:2]).then_inc(h2_done, 1)

            def first_out(c):
                need(act, t1_done, c)
                need(act, cmr_done, c, 1)
                need(act, cmi_done, c, 1)
                act.copy(xf[:, :, :], ps[:, 2:4]).then_inc(xf_done, 1)
                need(act, xf_done, c)
                act.copy(xh[:, :, :], xf[:, :, :]).then_inc(xh_done, 1)

            def relu(c, m):
                need_block(act, f1_done, m, c)
                if m >= SLOTS:
                    need_block(act, rl_done, m - SLOTS, c)
                else:
                    need_block(act, rl_done, m + SLOTS, c, 1)
                act.activation(rf[:, m % SLOTS], ps[:, 6 + m % 2], ACT.Relu, scale=relu_scale[:, 0:1],
                               bias=relu_bias[:, m:m + 1]).then_inc(relu_done[m % SLOTS], 1)

            def relu_hi(c, m):
                need_block(act, relu_done, m, c)
                if m >= SLOTS:
                    need_block(act, f2_done, m - SLOTS, c)
                else:
                    need_block(act, f2_done, m + SLOTS, c, 1)
                act.copy(rh[:, m % SLOTS], rf[:, m % SLOTS]).then_inc(rh_done[m % SLOTS], 1)

            def step(s):
                now, nxt, ahead, far = s.chunk(0), s.chunk(1), s.chunk(2), s.chunk(3)
                if ahead and now:
                    omega_out(ahead)
                if ahead:
                    sin_cos(ahead)
                    base_scaled(ahead)
                    context_hi(ahead, 0, cmr_done, cmr[:, :, :])
                    context_hi(ahead, 1, cmi_done, cmi[:, :, :])
                if now:
                    second_hi(now)
                if nxt:
                    spread_out(nxt)
                    gelu(nxt, 0)
                    gelu(nxt, 1)
                if nxt:
                    gelu(nxt, 2)
                if nxt and not now:
                    gelu(nxt, 3)
                for m in range(KF):
                    if now:
                        relu(now, m)
                        if m:
                            relu_hi(now, m - 1)
                    if m == 3 and nxt and now:
                        gelu(nxt, 3)
                    if m == 4 and ahead:
                        square_real(ahead)
                    if m == 5 and far:
                        first_out(far)
                    if m == 6 and ahead:
                        square_imag(ahead)
                if now:
                    relu_hi(now, KF - 1)
                if ahead:
                    context_hi(ahead, 2, rr_done, rr[:, :, :])
                    context_hi(ahead, 3, ri_done, ri[:, :, :])
                    sums_hi(ahead)

            def group_hi(n):
                tiles, hi, lo, scale = groups[n]
                act.wait_ge(p_turned, n + 1)
                if lo is None:
                    act.copy(hi, ps[:, group_banks[n], :]).then_inc(p_plain, 1)
                else:
                    act.activation(hi, ps[:, group_banks[n], :], ACT.Copy,
                                   scale=up[:, scale:scale + 1]).then_inc(p_hi, 1)

            first, second = first_chunks(act)
            act.wait_ge(p_scales, 1)
            group_hi(0)
            first_out(first)
            dump = base[:, :, :, :].rearrange("p b t d -> p (b t d)")
            for i, (s, w) in enumerate(((p_fw1, fw1_in), (p_fw2, fw2_in))):
                act.wait_ge(s, 16)
                if i:
                    act.wait_ge(p_abs, i)
                act.activation(dump, w.rearrange("p m d -> p (m d)"), ACT.Abs,
                               accum_out=abs_sums[:, i:i + 1]).then_inc(p_abs, 1)
            act.wait_ge(p_scales, 2)
            omega_out(first)
            act.wait_ge(p_abs, 2)
            for m in range(KE):
                act.wait_ge(p_gamma, m + 1)
                if m >= 2:
                    act.wait_ge(p_rows, m - 1)
                act.activation(dump[:, (m % 2) * C:(m % 2 + 1) * C], w1_in[:, m], ACT.Copy,
                               accum_out=row_mean[:, m:m + 1]).then_inc(p_rows, 1)
            act.wait_ge(p_rows, KE)
            act.activation(minus_mean[:, :], row_mean[:, :], ACT.Copy, scale=-1.0 / C).then_inc(p_rows, 1)
            sin_cos(first)
            act.wait_ge(p_rows, KE + 1)
            for m in range(KE):
                if m >= 2:
                    act.wait_ge(p_squares, m - 1)
                act.activation(dump[:, (m % 2) * C:(m % 2 + 1) * C], w1_in[:, m], ACT.Square,
                               accum_out=row_squares[:, m:m + 1]).then_inc(p_squares, 1)
            act.wait_ge(p_squares, KE)
            for m in range(KE):
                act.activation(w1_in[:, m], w1_in[:, m], ACT.Identity,
                               bias=minus_mean[:, m:m + 1]).then_inc(p_fold, 1)
            base_scaled(first)
            for n in range(1, 1 + plain_upto[-1]):
                group_hi(n)
            square_real(first)
            context_hi(first, 0, cmr_done, cmr[:, :, :])
            context_hi(first, 1, cmi_done, cmi[:, :, :])
            square_imag(first)
            first_out(second)
            act.wait_ge(p_scales, 3)
            for n in range(1 + plain_upto[-1], len(groups)):
                group_hi(n)
            context_hi(first, 2, rr_done, rr[:, :, :])
            context_hi(first, 3, ri_done, ri[:, :, :])
            omega_out(second)
            sums_hi(first)
            prepared(act)
            run(act, step, -1)

        @block.tensor
        def _(pe):
            pe.wait_ge(p_ident, 1)
            pe.wait_ge(p_ones, 1)
            def first_transposes(c):
                need(pe, xs_done, c)
                need(pe, rbs_done, c, 2)
                need(pe, csq_done, c, 2)
                for k in range(KD):
                    for j in range(NT):
                        last = pe.transpose(ps[:, 2 + k, j * P:(j + 1) * P], xs[:, j, k * P:(k + 1) * P], ident[:, :])
                last.then_inc(t1_done, 1)

            def omega(c):
                need(pe, xh_done, c)
                need(pe, xl_done, c)
                for e in range(KD):
                    passes = [(w, a, k) for w, a in ((wo_hi, xh), (wo_hi, xl), (wo_lo, xh)) for k in range(KD)]
                    for i, (w, a, k) in enumerate(passes):
                        last = pe.matmul(ps[:, 2 + e], w[:, k, e * P:(e + 1) * P], a[:, k],
                                         start=(i == 0), stop=(i == len(passes) - 1))
                last.then_inc(omega_done, 1)

            def context_stats(c, after):
                for half_done in (qh_done, ql_done, sh_done, sl_done):
                    need(pe, half_done, c)
                if after:
                    need(pe, w_done, after)
                for i, halves in enumerate(((s_hi, s_lo), (q_hi, q_lo))):
                    for j in range(NT):
                        col = i * NT + j
                        for src in halves:
                            last = pe.matmul(ps[:, 3, col:col + 1], src[:, j * P:(j + 1) * P], ones_h[:, 0:1],
                                             start=(src is halves[0]), stop=(src is halves[1]))
                last.then_inc(stats_done, 1)

            def spread(c):
                need(pe, diag_hi_done, c)
                need(pe, diag_done, c)
                pe.matmul(ps[:, 2], ones_h[:, :], diag_hi[:, :, :], start=True, stop=False)
                pe.matmul(ps[:, 2], ones_h[:, :], diag_lo[:, :, :], start=False, stop=True).then_inc(spread_done, 1)

            def hidden(c, m):
                if m < 2:
                    need(pe, x1_done, c, 1)
                else:
                    need_block(pe, relu_done, KF - 4 + m, c, 2)
                if m == 0:
                    for part in range(4):
                        need(pe, ch_done[part], c)
                        need(pe, cl_done[part], c)
                passes = [(w, a, k) for k in range(KC) for w, a in ((w1_hi, ch), (w1_hi, cl), (w1_lo, ch))]
                for i, (w, a, k) in enumerate(passes):
                    last = pe.matmul(ps[:, 4 + m], w[:, k, m * P:(m + 1) * P], a[:, c.b, k],
                                     start=(i == 0), stop=(i == len(passes) - 1))
                last.then_inc(w1_done[m], 1)

            def second_transposes(c):
                need(pe, xs2_done, c)
                need(pe, out_done, c, 1)
                for k in range(KD):
                    for j in range(NT):
                        last = pe.transpose(ps[:, k, j * P:(j + 1) * P], xs2[:, j, k * P:(k + 1) * P], ident[:, :])
                last.then_inc(t2_done, 1)

            def ffn_in(c, m, after):
                if m == 0:
                    need(pe, h2_done, c)
                    need(pe, l2_done, c)
                if m >= 2:
                    need_block(pe, relu_done, m - 2, c)
                elif after:
                    need(pe, z_done[2 + m], after)
                passes = [(a, k) for k in range(KD) for a in (h2, l2)]
                for i, (a, k) in enumerate(passes):
                    last = pe.matmul(ps[:, 6 + m % 2], fw1_t[:, k, m * P:(m + 1) * P], a[:, k],
                                     start=(i == 0), stop=(i == len(passes) - 1))
                last.then_inc(f1_done[m % SLOTS], 1)

            def ffn_out(c, m):
                need_block(pe, rh_done, m, c)
                need_block(pe, rl_done, m, c)
                for j in range(NT):
                    for a in (rh, rl):
                        last = pe.matmul(ps_rows_a[:, j], a[:, m % SLOTS, j * P:(j + 1) * P], fw2_t[:, m],
                                         start=(m == 0 and j % 2 == 0 and a is rh), stop=(m == KF - 1 and a is rl),
                                         skip_group_check=True)
                last.then_inc(f2_done[m % SLOTS], 1)

            def mixer_out(c):
                for m in range(KE):
                    need(pe, gh_done[m], c)
                    need(pe, gl_done[m], c)
                for j in range(NT):
                    passes = [(a, w, m) for m in range(KE) for a, w in ((gh, w2_hi), (gh, w2_lo), (gl, w2_hi))]
                    for i, (a, w, m) in enumerate(passes):
                        last = pe.matmul(ps_rows_b[:, j], a[:, m, j * P:(j + 1) * P], w[:, m],
                                         start=(i == 0), stop=(i == len(passes) - 1))
                last.then_inc(w2_done, 1)

            def step(s):
                now, nxt, ahead, far = s.chunk(0), s.chunk(1), s.chunk(2), s.chunk(3)
                if ahead and now:
                    omega(ahead)
                if nxt:
                    hidden(nxt, 0)
                    context_stats(nxt, ahead)
                    hidden(nxt, 1)
                if now:
                    second_transposes(now)
                if nxt:
                    hidden(nxt, 2)
                    spread(nxt)
                    hidden(nxt, 3)
                for m in range(KF):
                    if now:
                        ffn_in(now, m, nxt)
                        if m >= LAG:
                            ffn_out(now, m - LAG)
                    if m == 2 and far:
                        first_transposes(far)
                if nxt:
                    mixer_out(nxt)
                if now:
                    for m in range(KF - LAG, KF):
                        ffn_out(now, m)

            def turn_group(n):
                tiles, hi, lo, scale = groups[n]
                if scale == 0:
                    pe.wait_ge(p_wo, 16)
                elif scale == 1:
                    pe.wait_ge(p_fold, KE)
                elif scale == 2:
                    pe.wait_ge(p_w2, 16)
                else:
                    pe.wait_ge(p_tern, 2)
                if n >= 6:
                    group_out(pe, n - 6)
                for q, (src, m, k) in enumerate(tiles):
                    last = pe.transpose(ps[:, group_banks[n], q * P:(q + 1) * P], src[:, m, k * P:(k + 1) * P],
                                        ident[:, :])
                last.then_inc(p_turned, 1)

            first, second = first_chunks(pe)
            turn_group(0)
            first_transposes(first)
            pe.wait_ge(p_lo, 1)
            omega(first)
            pe.wait_ge(p_abs, 2)
            pe.matmul(ps[:, 7, 0:2], ones[:, 0:P], abs_sums[:, :], start=True, stop=True).then_inc(p_mean, 1)
            for n in range(1, 1 + plain_upto[-1]):
                turn_group(n)
            first_transposes(second)
            split_from = 1 + plain_upto[-1]
            for n in range(split_from, split_from + 6):
                turn_group(n)
            omega(second)
            for n in range(split_from + 6, len(groups)):
                turn_group(n)
            prepared(pe)
            run(pe, step, -1)

        @block.vector
        def _(dve):
            done = [0]

            def link(ins):
                done[0] += 1
                ins.then_inc(p_dve, 1)
                dve.wait_ge(p_dve, done[0])

            dve.memset(ones_h[:, :], 1.0)
            dve.memset(ones[:, :], 1.0).then_inc(p_ones, 1)
            link(dve.memset(half_pi[:, :], PI / 2))
            def statistics_1(c):
                need_dma(dve, x_loaded, c)
                need(dve, mv1_done, c, 1)
                for j in range(NT):
                    last = dve.bn_stats(bn1[:, j], x_rows[:, c.b, j])
                last.then_inc(bn1_done, 1)
                stand_alone(dve)
                need(dve, bn1_done, c)
                need(dve, base_done, c, 2)
                for j in range(NT):
                    last = dve.bn_aggr(mv1[:, c.b, j], bn1[:, j])
                last.then_inc(mv1_done, 1)
                need(dve, mv1_done, c)
                need(dve, rs1_done, c, 1)
                dve.tensor_scalar(ve1[:, :], mv1[:, c.b, :, 1], EPS, LN_SCALE ** -2, ALU.add, ALU.mult)\
                   .then_inc(ve1_done, 1)

            def normalise_1(c):
                need(dve, t1_done, c, 1)
                need(dve, rs1_done, c)
                for j in range(NT):
                    last = dve.tensor_scalar(xs[:, j], x_rows[:, c.b, j], mv1[:, c.b, j, 0:1],
                                             rs1[:, c.b, j:j + 1], ALU.subtract, ALU.mult)
                last.then_inc(xs_done, 1)

            def normalise_2(c):
                need(dve, t2_done, c, 1)
                need(dve, rs2_done, c)
                for j in range(NT):
                    last = dve.tensor_scalar(xs2[:, j], x1[:, c.b, j], mv2[:, j, 0:1], rs2[:, j:j + 1],
                                             ALU.subtract, ALU.mult)
                last.then_inc(xs2_done, 1)

            def gains_1(c):
                need(dve, rs1_done, c)
                dve.tensor_scalar(gain1[:, c.b], rs1[:, c.b], 1.0 / LN_SCALE, 1.0, ALU.mult, ALU.add)
                dve.scalar_tensor_tensor(out=shift1[:, c.b], in0=rs1[:, c.b], scalar=-1.0 / LN_SCALE,
                                         in1=mv1[:, c.b, :, 0], op0=ALU.mult, op1=ALU.mult).then_inc(gain_done, 1)
                dve.scalar_tensor_tensor(out=sq1[:, c.b], in0=rs1[:, c.b], scalar=float(D),
                                         in1=mv1[:, c.b, :, 1], op0=ALU.mult, op1=ALU.mult).then_inc(sq1a_done, 1)
                need(dve, sq1a_done, c)
                dve.tensor_tensor(sq1[:, c.b], sq1[:, c.b], rs1[:, c.b], ALU.mult).then_inc(sq1_done, 1)

            def first_lo(c):
                need(dve, xh_done, c)
                need(dve, omega_done, c, 1)
                dve.tensor_tensor(xl[:, :, :], xf[:, :, :], xh[:, :, :], ALU.subtract).then_inc(xl_done, 1)

            def phase(c):
                need(dve, w_done, c)
                table = pos_rsqrt[:, c.b * CH:(c.b + 1) * CH].unsqueeze(1).to_broadcast([P, KD, CH])
                dve.tensor_tensor(ph[:, :, :], ph[:, :, :], table, ALU.mult).then_inc(u_done, 1)
                need(dve, u_done, c)
                need(dve, ycarry_done, c, 1)
                for k in range(KD):
                    last = dve.tensor_tensor_scan(ph[:, k], ones[:, 0:1].to_broadcast([P, CH]), ph[:, k],
                                                  ph_carry[:, k] if c.b else 0.0, ALU.mult, ALU.add)
                last.then_inc(y_done, 1)
                need(dve, y_done, c)
                dve.tensor_copy(ph_carry[:, :, :], ph[:, :, CH - 1:CH]).then_inc(ycarry_done, 1)
                need(dve, q2_done, c, 1)
                dve.tensor_scalar(turn[:, :, :], ph[:, :, :], ROUND, ROUND, ALU.add, ALU.subtract)\
                   .then_inc(turn_done, 1)
                need(dve, turn_done, c)
                need(dve, ycarry_done, c)
                dve.tensor_tensor(ph[:, :, :], ph[:, :, :], turn[:, :, :], ALU.subtract).then_inc(frac_done, 1)

            def modulate(c):
                need(dve, cos_done, c)
                need(dve, stats_done, c, 1)
                dve.tensor_tensor(cmr[:, :, :], xf[:, :, :], cs[:, :, :], ALU.mult).then_inc(cmr_done, 1)
                need(dve, s2_done, c, 1)
                dve.tensor_tensor(cmi[:, :, :], xf[:, :, :], sn[:, :, :], ALU.mult).then_inc(cmi_done, 1)

            def prefix_sums(c):
                need(dve, cmi_done, c)
                need(dve, sqi_done, c, 1)
                need(dve, rcarry_done, c, 1)
                need(dve, icarry_done, c, 1)
                for k in range(KD):
                    last = dve.tensor_tensor_scan(mi[:, k], ones[:, 0:1].to_broadcast([P, CH]), cmi[:, k],
                                                  mi_carry[:, k] if c.b else 0.0, ALU.mult, ALU.add)
                last.then_inc(sumi_done, 1)
                for k in range(KD):
                    last = dve.tensor_tensor_scan(mr[:, k], ones[:, 0:1].to_broadcast([P, CH]), cmr[:, k],
                                                  mr_carry[:, k] if c.b else 0.0, ALU.mult, ALU.add)
                last.then_inc(sumr_done, 1)
                need(dve, sumi_done, c)
                dve.tensor_copy(mi_carry[:, :, :], mi[:, :, CH - 1:CH]).then_inc(icarry_done, 1)
                need(dve, sumr_done, c)
                dve.tensor_copy(mr_carry[:, :, :], mr[:, :, CH - 1:CH]).then_inc(rcarry_done, 1)

            def memory_real(c):
                need(dve, rcarry_done, c)
                table = pos_inv[:, c.b * CH:(c.b + 1) * CH].unsqueeze(1).to_broadcast([P, KD, CH])
                dve.tensor_tensor(mr[:, :, :], mr[:, :, :], table, ALU.mult).then_inc(mr_done, 1)

            def retrieve_real_cos(c):
                need(dve, mr_done, c)
                need(dve, s3_done, c, 1)
                dve.tensor_tensor(rr[:, :, :], mr[:, :, :], cs[:, :, :], ALU.mult).then_inc(ra_done, 1)

            def retrieve_imag_cos(c):
                need(dve, mi_done, c)
                need(dve, s4_done, c, 1)
                dve.tensor_tensor(ri[:, :, :], mi[:, :, :], cs[:, :, :], ALU.mult).then_inc(rb_done, 1)

            def retrieve(c):
                need(dve, ra_done, c)
                need(dve, qa_done, c)
                dve.tensor_tensor(rr[:, :, :], rr[:, :, :], qa[:, :, :], ALU.add).then_inc(rr_done, 1)

            def context_lo(c, part, src):
                need(dve, ch_done[part], c)
                need(dve, w1_done[KE - 1], c, 2)
                dve.tensor_tensor(cl[:, c.b, 2 * part:2 * part + 2], src, ch[:, c.b, 2 * part:2 * part + 2],
                                  ALU.subtract).then_inc(cl_done[part], 1)

            def context_variance(c):
                need(dve, stats_done, c)
                dve.tensor_scalar(cmu[:, :], ps[:, 3, 0:NT], 1.0 / (RSTD_SCALE * C), None, ALU.mult).then_inc(cmu_done, 1)
                need(dve, sq1_done, c)
                dve.scalar_tensor_tensor(out=csq[:, :], in0=ps[:, 3, NT:2 * NT], scalar=SQUARE_SCALE ** -2,
                                         in1=sq1[:, c.b], op0=ALU.mult, op1=ALU.add).then_inc(csq_done, 1)
                need(dve, cmu_done, c)
                dve.tensor_tensor(cmu2[:, :], cmu[:, :], cmu[:, :], ALU.mult).then_inc(cmu2_done, 1)
                need(dve, cmu2_done, c)
                need(dve, csq_done, c)
                dve.scalar_tensor_tensor(out=cvar[:, :], in0=csq[:, :], scalar=RSTD_SCALE ** -2 / C, in1=cmu2[:, :],
                                         op0=ALU.mult, op1=ALU.subtract).then_inc(cvar_done, 1)
                need(dve, cvar_done, c)
                need(dve, crs_done, c, 1)
                dve.tensor_scalar(cve[:, :], cvar[:, :], 0.0, EPS * (LN_SCALE / RSTD_SCALE) ** 2, ALU.max, ALU.add)\
                   .then_inc(cve_done, 1)

            def diagonal(c):
                need(dve, diag_hi_done, c)
                need(dve, spread_done, c, 1)
                for j in range(NT):
                    last = dve.scalar_tensor_tensor(out=diag_lo[:, j], in0=ident[:, :], scalar=crs[:, j:j + 1],
                                                    in1=diag_hi[:, j], op0=ALU.mult, op1=ALU.subtract)
                last.then_inc(diag_done, 1)

            def scale_hidden(c, m):
                need(dve, w1_done[m], c)
                need(dve, rbs_done, c)
                need(dve, gl_done[m], c, 1)
                dve.tensor_tensor(z[:, m], ps[:, 4 + m], rb[:, :], ALU.mult).then_inc(z_done[m], 1)

            def gelu_lo(c, m):
                need(dve, gh_done[m], c)
                need(dve, w2_done, c, 1)
                dve.scalar_tensor_tensor(out=gl[:, m], in0=z[:, m], scalar=up[:, 3:4], in1=gh[:, m],
                                         op0=ALU.mult, op1=ALU.subtract).then_inc(gl_done[m], 1)

            def mixer_residual(c):
                need(dve, w2_done, c)
                need(dve, base_done, c)
                need_dma(dve, stored, c, 2)
                dve.scalar_tensor_tensor(out=x1[:, c.b], in0=ps_rows_b, scalar=h_down[:, 0:1], in1=base[:, c.b],
                                         op0=ALU.mult, op1=ALU.add).then_inc(x1_done, 1)

            def statistics_2(c):
                need(dve, x1_done, c)
                need(dve, xs2_done, c, 1)
                for j in range(NT):
                    last = dve.bn_stats(bn2[:, j], x1[:, c.b, j])
                last.then_inc(bn2_done, 1)
                stand_alone(dve)
                need(dve, bn2_done, c)
                for j in range(NT):
                    last = dve.bn_aggr(mv2[:, j], bn2[:, j])
                last.then_inc(mv2_done, 1)
                need(dve, mv2_done, c)
                need(dve, rs2_done, c, 1)
                dve.tensor_scalar(ve2[:, :], mv2[:, :, 1], EPS, LN_SCALE ** -2, ALU.add, ALU.mult)\
                   .then_inc(ve2_done, 1)

            def second_lo(c):
                need(dve, h2_done, c)
                need_block(dve, f1_done, KF - 1, c, 1)
                dve.tensor_tensor(l2[:, :, :], ps[:, 0:2], h2[:, :, :], ALU.subtract).then_inc(l2_done, 1)

            def relu_lo(c, m):
                need_block(dve, rh_done, m, c)
                if m >= SLOTS:
                    need_block(dve, f2_done, m - SLOTS, c)
                else:
                    need_block(dve, f2_done, m + SLOTS, c, 1)
                dve.tensor_tensor(rl[:, m % SLOTS], rf[:, m % SLOTS], rh[:, m % SLOTS], ALU.subtract)\
                   .then_inc(rl_done[m % SLOTS], 1)

            def output(c):
                need_block(dve, f2_done, KF - 1, c)
                need(dve, xb_done, c)
                dve.scalar_tensor_tensor(out=x1[:, c.b], in0=ps_rows_a, scalar=down[:, 4:5], in1=x1[:, c.b],
                                         op0=ALU.mult, op1=ALU.add).then_inc(out_done, 1)

            def step(s):
                now, nxt, ahead, far = s.chunk(0), s.chunk(1), s.chunk(2), s.chunk(3)
                if now:
                    statistics_2(now)
                if ahead:
                    phase(ahead)
                if now:
                    normalise_2(now)
                if ahead and not now:
                    modulate(ahead)
                if nxt:
                    context_variance(nxt)
                if far:
                    statistics_1(far)
                if ahead and now:
                    modulate(ahead)
                if nxt:
                    diagonal(nxt)
                if ahead:
                    prefix_sums(ahead)
                    memory_real(ahead)
                if nxt:
                    scale_hidden(nxt, 0)
                    scale_hidden(nxt, 1)
                    scale_hidden(nxt, 2)
                if now:
                    second_lo(now)
                if ahead and not now:
                    retrieve_real_cos(ahead)
                if far:
                    normalise_1(far)
                if nxt:
                    scale_hidden(nxt, 3)
                if ahead and now:
                    retrieve_real_cos(ahead)
                if ahead:
                    retrieve_imag_cos(ahead)
                if ahead and not now:
                    context_lo(ahead, 0, cmr[:, :, :])
                if nxt and not now:
                    for m in range(KE):
                        gelu_lo(nxt, m)
                for m in range(KF):
                    if now:
                        relu_lo(now, m)
                    if m == 0 and nxt and now:
                        gelu_lo(nxt, 0)
                        gelu_lo(nxt, 1)
                    if m == 1 and ahead and now:
                        context_lo(ahead, 0, cmr[:, :, :])
                    if m == 2 and ahead:
                        retrieve(ahead)
                    if m == 3 and nxt and now:
                        gelu_lo(nxt, 2)
                        gelu_lo(nxt, 3)
                    if m == 4 and ahead:
                        context_lo(ahead, 1, cmi[:, :, :])
                    if m == 4 and far:
                        gains_1(far)
                    if m == 5 and far:
                        first_lo(far)
                if ahead:
                    context_lo(ahead, 2, rr[:, :, :])
                    context_lo(ahead, 3, ri[:, :, :])
                if nxt:
                    mixer_residual(nxt)
                if now:
                    output(now)

            def powers(cols):
                link(dve.tensor_scalar(pw[:, cols], pw[:, cols], 1e-30, None, ALU.max))
                link(dve.tensor_scalar(pw[:, cols].bitcast(U32), pw[:, cols].bitcast(U32), EXPONENT_BITS, None,
                                       ALU.bitwise_and))
                link(dve.reciprocal(up[:, cols], pw[:, cols]))
                link(dve.tensor_scalar(up[:, cols], up[:, cols], 2.0 ** 14, None, ALU.mult))
                return dve.tensor_scalar(down[:, cols], pw[:, cols], 2.0 ** -14, None, ALU.mult)

            def group_lo(n):
                tiles, hi, lo, scale = groups[n]
                dve.wait_ge(p_hi, scaled_upto[n])
                dve.scalar_tensor_tensor(out=lo, in0=ps[:, group_banks[n], :], scalar=up[:, scale:scale + 1],
                                         in1=hi, op0=ALU.mult, op1=ALU.subtract).then_inc(p_lo, 1)

            first, second = first_chunks(dve)
            dve.wait_ge(p_wo, 16)
            dve.tensor_reduce(mags[:, 0:1], wo_in, AX.XY, ALU.max, apply_absolute_value=True).then_inc(p_mags, 1)
            statistics_1(first)
            dve.wait_ge(p_max, 1)
            link(dve.tensor_copy(pw[:, 0:1], mags_all[:, 0:1]))
            powers(slice(0, 1)).then_inc(p_scales, 1)
            dve.wait_ge(p_scales, 1)
            normalise_1(first)
            dve.wait_ge(p_exp, 1)
            link(dve.tensor_scalar(om_scale[:, :], exp_ls[:, :], down[:, 0:1], 1.0 / (2 * PI * LN_SCALE),
                                   ALU.mult, ALU.mult))
            link(dve.tensor_tensor(om_bias[:, :], exp_ls[:, :], b_om[:, :], ALU.mult))
            dve.tensor_scalar(om_bias[:, :], om_bias[:, :], 1.0 / (2 * PI), None, ALU.mult).then_inc(p_scales, 1)
            group_lo(0)
            gains_1(first)
            first_lo(first)
            dve.wait_ge(p_vec, 32)
            dve.tensor_reduce(mags[:, 4:5], fb1[:, :], AX.X, ALU.max,
                              apply_absolute_value=True).then_inc(p_mags, 1)
            dve.wait_ge(p_w1, 48)
            for m in range(KE):
                dve.tensor_tensor_reduce(w_tmp[:, 0:C], w1_in[:, m], beta_rows, 1.0, 0.0, ALU.mult, ALU.add,
                                         b1_dot[:, m:m + 1]).then_inc(p_dot, 1)
                dve.wait_ge(p_dot, m + 1)
            link(dve.tensor_tensor(b1_full[:, :], b1_dot[:, :], b1_raw[:, :], ALU.add))
            dve.tensor_reduce(mags[:, 3:4], b1_full[:, :], AX.X, ALU.max,
                              apply_absolute_value=True).then_inc(p_mags, 1)
            dve.wait_ge(p_w2, 16)
            dve.tensor_reduce(mags[:, 2:3], w2_in, AX.XY, ALU.max,
                              apply_absolute_value=True).then_inc(p_mags, 1)
            dve.wait_ge(p_pos, 16)
            phase(first)
            statistics_1(second)
            dve.wait_ge(p_mean, 1)
            link(dve.tensor_scalar(thr[:, :], ps[:, 7, 0:2], 1.0 / (F * D), EPS, ALU.mult, ALU.add))
            link(dve.tensor_scalar(neg_thr[:, :], thr[:, :], -0.5, None, ALU.mult))
            link(dve.tensor_scalar(thr[:, :], thr[:, :], 0.5, None, ALU.mult))
            for i, w in enumerate((fw1_in, fw2_in)):
                flat = w.rearrange("p m d -> p (m d)")
                link(dve.tensor_scalar(w_tmp, flat, neg_thr[:, i:i + 1], None, ALU.is_lt))
                dve.scalar_tensor_tensor(out=flat, in0=flat, scalar=thr[:, i:i + 1], in1=w_tmp, op0=ALU.is_gt,
                                         op1=ALU.subtract).then_inc(p_tern, 1)
                dve.wait_ge(p_tern, i + 1)
            dve.wait_ge(p_squares, KE)
            dve.tensor_reduce(mags[:, 1:2], row_squares[:, :], AX.X, ALU.max).then_inc(p_mags, 1)
            modulate(first)
            prefix_sums(first)
            dve.wait_ge(p_tab, 48)
            memory_real(first)
            dve.wait_ge(p_max, 3)
            link(dve.tensor_copy(pw[:, 1:3], mags_all[:, 1:3]))
            link(dve.scalar_tensor_tensor(out=pw[:, 3:4], in0=mags_all[:, 1:2], scalar=C ** 0.5,
                                          in1=mags_all[:, 3:4], op0=ALU.mult, op1=ALU.add))
            link(dve.tensor_scalar(pw[:, 4:5], mags_all[:, 4:5], float(D), None, ALU.add))
            link(powers(slice(1, 5)))
            dve.tensor_tensor(h_down[:, :], down[:, 2:3], down[:, 3:4], ALU.mult)
            dve.tensor_scalar(z_down[:, :], down[:, 1:2], 1.0 / RSTD_SCALE, None, ALU.mult)
            link(dve.tensor_scalar(relu_scale[:, :], up[:, 4:5], 1.0 / LN_SCALE, None, ALU.mult))
            dve.tensor_scalar(relu_bias[:, :], fb1[:, :], up[:, 4:5], None, ALU.mult).then_inc(p_scales, 1)
            normalise_1(second)
            retrieve_real_cos(first)
            retrieve_imag_cos(first)
            context_lo(first, 0, cmr[:, :, :])
            gains_1(second)
            retrieve(first)
            first_lo(second)
            context_lo(first, 1, cmi[:, :, :])
            for n in range(1, len(groups)):
                if groups[n][2] is not None:
                    group_lo(n)
            context_lo(first, 2, rr[:, :, :])
            context_lo(first, 3, ri[:, :, :])
            prepared(dve)
            run(dve, step, -1)


_INS = ['L0_attn_x', 'L0_attn_W_omega', 'L0_attn_b_omega', 'L0_attn_log_scale', 'L0_attn_ln_gamma',
        'L0_attn_ln_beta', 'L0_attn_W1', 'L0_attn_b1', 'L0_attn_W2', 'L0_attn_b2',
        'L0_ffn_W1', 'L0_ffn_b1', 'L0_ffn_W2', 'L0_ffn_b2']


def kernel(**inputs):
    import numpy as np
    import concourse.bacc as bacc
    from concourse.bass_utils import run_bass_kernel_spmd

    nc = bacc.Bacc("TRN2", target_bir_lowering=False, num_devices=1)
    arrays, args = {}, []
    for name in _INS:
        a = np.ascontiguousarray(inputs[name])
        arrays[f"in_{name}"] = a
        args.append(nc.dram_tensor(f"in_{name}", a.shape, mybir.dt.from_np(a.dtype), kind="ExternalInput").ap())
    shape = inputs['L0_attn_x'].shape
    position = np.arange(1, shape[1] + 1, dtype=np.float32)
    table = np.stack([np.float32(1) / np.sqrt(position), np.float32(1) / position]).astype(np.float32)
    arrays["in_positions"] = table
    args.append(nc.dram_tensor("in_positions", table.shape, F32, kind="ExternalInput").ap())
    args.append(nc.dram_tensor("out_0", shape, F32, kind="ExternalOutput").ap())
    phase_mixer_layer(nc, *args)
    r = run_bass_kernel_spmd(nc, [arrays], core_ids=[0])
    return r.results[0]["out_0"]
```
